# Optimizing a Trainium2 kernel written in Bass

```python
import numpy as np
import jax
import jax.numpy as jnp

def _softmax(x, axis=-1):
    return jax.nn.softmax(x, axis=axis)

def _gelu(x):
    return jax.nn.gelu(x, approximate=True)

def _silu(x):
    return jax.nn.silu(x)

def _sigmoid(x):
    return jax.nn.sigmoid(x)

def _layernorm(x, axis=-1, eps=1e-05):
    m = jnp.mean(x, axis=axis, keepdims=True)
    v = jnp.var(x, axis=axis, keepdims=True)
    return (x - m) / jnp.sqrt(v + eps)

def _scatter_add(tgt, idx, src, axis=0):
    return tgt.at[idx].add(src)

def _segment_sum(src, seg, n):
    return jax.ops.segment_sum(src, seg, n)
kernel_name = 'mk_seq_postln_d1_jaxref_r8_9d4fdf'

def setup_inputs(seed: int=0):
    np.random.seed(seed)
    _w = jnp.asarray

    def _L0_attn_setup():
        import jax, jax.numpy as jnp
        import numpy as np
        B, T, C = (2, 256, 256)
        N_HEAD = 16
        HS = C // N_HEAD
        D_LATENT = C // 2
        key = jax.random.key(seed)
        ks = jax.random.split(key, 7)
        s = 0.02
        return {'x': jax.random.normal(ks[0], (B, T, C), dtype=jnp.float32), 'Wq': jax.random.normal(ks[1], (C, C), dtype=jnp.float32) * s, 'Wc': jax.random.normal(ks[2], (C, D_LATENT), dtype=jnp.float32) * s, 'Wk': jax.random.normal(ks[3], (D_LATENT, C), dtype=jnp.float32) * s, 'Wv': jax.random.normal(ks[4], (D_LATENT, C), dtype=jnp.float32) * s, 'Wo': jax.random.normal(ks[5], (C, C), dtype=jnp.float32) * s, 'bo': jnp.zeros((C,), dtype=jnp.float32)}
    _L0_attn_in = _L0_attn_setup()

    def _L0_ffn_setup():
        import jax, jax.numpy as jnp
        import numpy as np
        H, I, E = (256, 512, 8)
        B, S = (2, 256)
        key = jax.random.key(seed)
        ks = jax.random.split(key, 5)
        scale = 0.02
        return {'hidden_states': jax.random.normal(ks[0], (B, S, H), dtype=jnp.float32), 'router_w': jax.random.normal(ks[1], (H, E), dtype=jnp.float32) * scale, 'gate_w': jax.random.normal(ks[2], (E, H, I), dtype=jnp.float32) * scale, 'up_w': jax.random.normal(ks[3], (E, H, I), dtype=jnp.float32) * scale, 'down_w': jax.random.normal(ks[4], (E, I, H), dtype=jnp.float32) * scale}
    _L0_ffn_in = _L0_ffn_setup()
    _d = {'L0_attn_x': _L0_attn_in['x'], 'L0_attn_Wq': _L0_attn_in['Wq'], 'L0_attn_Wc': _L0_attn_in['Wc'], 'L0_attn_Wk': _L0_attn_in['Wk'], 'L0_attn_Wv': _L0_attn_in['Wv'], 'L0_attn_Wo': _L0_attn_in['Wo'], 'L0_attn_bo': _L0_attn_in['bo'], 'L0_ffn_router_w': _L0_ffn_in['router_w'], 'L0_ffn_gate_w': _L0_ffn_in['gate_w'], 'L0_ffn_up_w': _L0_ffn_in['up_w'], 'L0_ffn_down_w': _L0_ffn_in['down_w']}
    _x0 = _d['L0_attn_x']
    _d['L0_attn_x'] = jax.random.normal(jax.random.fold_in(jax.random.key(seed), 1), (4, 512, 256), dtype=_x0.dtype)
    del _x0
    return _d

def reference(L0_attn_x, L0_attn_Wq, L0_attn_Wc, L0_attn_Wk, L0_attn_Wv, L0_attn_Wo, L0_attn_bo, L0_ffn_router_w, L0_ffn_gate_w, L0_ffn_up_w, L0_ffn_down_w):

    def _L0_attn_ref(x, Wq, Wc, Wk, Wv, Wo, bo):
        import jax, jax.numpy as jnp
        import numpy as np
        B, T, C = (2, 256, 256)
        N_HEAD = 16
        HS = C // N_HEAD
        D_LATENT = C // 2
        b, t, c = x.shape
        q = x @ Wq
        c_latent = x @ Wc
        k = c_latent @ Wk
        v = c_latent @ Wv
        q = q.reshape(b, t, N_HEAD, HS).transpose(0, 2, 1, 3)
        k = k.reshape(b, t, N_HEAD, HS).transpose(0, 2, 1, 3)
        v = v.reshape(b, t, N_HEAD, HS).transpose(0, 2, 1, 3)
        scale = 1.0 / jnp.sqrt(jnp.asarray(HS, dtype=x.dtype))
        scores = jnp.einsum('bhqd,bhkd->bhqk', q, k) * scale
        causal = jnp.tril(jnp.ones((t, t), dtype=bool))
        scores = jnp.where(causal, scores, jnp.finfo(scores.dtype).min)
        attn = jax.nn.softmax(scores, axis=-1)
        y = jnp.einsum('bhqk,bhkd->bhqd', attn, v)
        y = y.transpose(0, 2, 1, 3).reshape(b, t, c)
        return y @ Wo + bo

    def _L0_ffn_ref(hidden_states, router_w, gate_w, up_w, down_w):
        import jax, jax.numpy as jnp
        import numpy as np
        H, I, E = (256, 512, 8)
        B, S = (2, 256)
        hidden_shape = hidden_states.shape
        x = hidden_states.reshape(-1, hidden_shape[-1])
        route = jax.nn.sigmoid(x @ router_w)
        max_ind = jnp.argmax(route, axis=1)
        max_prob = jnp.take_along_axis(route, max_ind[:, None], axis=1)
        out = jnp.zeros_like(x)
        num_experts = gate_w.shape[0]
        for e in range(num_experts):
            mask = (max_ind == e)[:, None]
            h = jax.nn.silu(x @ gate_w[e]) * (x @ up_w[e])
            out = out + jnp.where(mask, h @ down_w[e], 0.0)
        out = out * max_prob
        return out.reshape(hidden_shape)
    x = L0_attn_x
    x = _layernorm(x + _L0_attn_ref(x, L0_attn_Wq, L0_attn_Wc, L0_attn_Wk, L0_attn_Wv, L0_attn_Wo, L0_attn_bo), axis=-1)
    x = _layernorm(x + _L0_ffn_ref(x, L0_ffn_router_w, L0_ffn_gate_w, L0_ffn_up_w, L0_ffn_down_w), axis=-1)
    return x

_drawn_inputs = setup_inputs


def setup_inputs(seed=0):
    import zlib

    import numpy as np

    out = dict(_drawn_inputs(seed))
    spreads = {'L0_attn_bo': (0.0, 0.1)}
    factors = {'L0_attn_Wq': 8.0,
     'L0_attn_Wc': 8.0,
     'L0_attn_Wk': 8.0,
     'L0_attn_Wv': 8.0,
     'L0_attn_Wo': 8.0,
     'L0_ffn_router_w': 4.152,
     'L0_ffn_gate_w': 3.899,
     'L0_ffn_up_w': 3.86,
     'L0_ffn_down_w': 3.86}
    for name, (base, spread) in spreads.items():
        noise = np.random.default_rng([zlib.crc32(name.encode()), seed]).standard_normal(out[name].shape)
        drawn = base * np.exp(spread * noise) if base else spread * noise
        out[name] = jnp.asarray(drawn.astype(out[name].dtype))
    for name, factor in factors.items():
        out[name] = (out[name] * factor).astype(out[name].dtype)
    return out
```

```python
import concourse.bass as bass
from concourse import mybir
from contextlib import ExitStack

F32 = mybir.dt.float32
BF16 = mybir.dt.bfloat16
I32 = mybir.dt.int32
ALU = mybir.AluOpType
ACT = mybir.ActivationFunctionType
AX = mybir.AxisListType

P = 128
NB, T, C = 4, 512, 256
NH, HS = 16, 16
NTOK = NB * T
TT = T // P
CC = C // P
GH = 4
NG = NH // GH
LAT = 128
NE, NI = 8, 512
IC = NI // P
TERMS = 6
KS = TERMS * HS
KM = KS + 3
Q_PART = [0, 0, 1, 1, 0, 2]
K_PART = [0, 1, 0, 1, 2, 0]
VW = HS + 1
SCORE_SCALE = HS ** -0.5
EPS = 1e-5
MASKED = -1e30
NT = NTOK // P + NE - 1
REGION = NTOK + P
PAD_ROW = NE * REGION
ROW = C + 2
NO_TOKEN = 4096.0
PAIRS = NT // 2
BANKS = 10


def steps_of(first, last):
    order = []
    for g in range(NG):
        before = not (first and g == 0)
        ahead = not (last and g >= 2)
        order += [("B", g, 0), ("B", g, 1)]
        order += [("PV", g, 2)] * before + [("V", g, 0)] * (g == 0)
        order += [("YT", g, 0)] * (g == 1 and not first)
        order += [("S", g, 0)] * ahead + [("B", g, 2), ("B", g, 3)]
        order += [("M", g, 0)] * (not (last and g == NG - 1))
        order += [("S", g, 1)] * ahead + [("B", g, 4), ("B", g, 5)]
        order += [("OT", g, 0)] * before + [("PV", g, 0)]
        order += [("S", g, 2)] * ahead + [("B", g, 6), ("B", g, 7)]
        order += [("S", g, 3)] * ahead
        if g == 0 and not last:
            order += [("X", g, 0), ("Q", g, 0)]
        if g == 2 and not first:
            order += [("LN", g, 0), ("X1T", g, 0)]
        if g == 3 and not first:
            order += [("RK", g, 0)]
        order += [("B", g, 8), ("B", g, 9)] + [("S", g, 4)] * ahead
        if g == 0 and not last:
            order += [("C", g, 0), ("K", g, 0)]
        if g == 1 and not first:
            order += [("WO", g, 0)]
        if g == 2 and not first:
            order += [("R", g, 0)]
        order += [("PV", g, 1)]
    return order


PROLOGUE = ([(x, -3, 0) for x in ("X", "Q", "C", "K")] + [("S", -2, u) for u in range(5)]
            + [("S", -1, 0), ("M", -1, 0)] + [("S", -1, u) for u in range(1, 5)])
EPILOGUE = [(x, NG, 2 * (x == "PV")) for x in ("PV", "OT", "YT", "WO", "LN", "X1T", "R", "RK")]
UNITS = ("X", "Q", "C", "K", "V", "S", "M", "OT", "YT", "WO", "X1T", "R", "RK")


def units_in(order):
    return sum(name in UNITS for name, _, _ in order)


def projected(b, g):
    return b + (g >= 0)


def past(b, g):
    return b + (g == NG)


def unit_numbers(order, wanted, n):
    names = [name for name, _, _ in order if name in UNITS]
    return [n + k for k, name in enumerate(names) if name == wanted]


def wait(engine, sem, value):
    if not isinstance(value, int) or value > 0:
        engine.wait_ge(sem, value)


class Chain:

    def __init__(self, engine, sem, per_body):
        self.engine, self.sem, self.per_body = engine, sem, per_body
        self.done, self.batch = 0, None

    def link(self, instruction):
        self.done += 1
        instruction.then_inc(self.sem, 1)
        more = 0 if self.batch is None else (self.batch - 1) * self.per_body
        self.engine.wait_ge(self.sem, self.done + more)

    def counted(self, run):
        def counted_run(b, order, const, per):
            in_loop = not isinstance(b, int)
            self.batch, began = (b if in_loop else None), self.done
            run(b, order, const, per)
            if in_loop:
                assert self.done - began == self.per_body, self.done - began
                self.done += (NB - 3) * self.per_body
            self.batch = None
        return counted_run


DVE_LINKS, POOL_LINKS = 28, 1


def kernel_program(nc, x, Wq, Wc, Wk, Wv, Wo, bo, router_w, gate_w, up_w, down_w, out):
    tokens = x.rearrange("b (t p) c -> p (b t) c", p=P)
    out_rows = out.rearrange("b t c -> (b t) c")
    first_body, middle_body, last_body = steps_of(True, False), steps_of(False, False), steps_of(False, True)
    U_MID = units_in(middle_body)
    U_START = units_in(PROLOGUE) + units_in(first_body)
    U0 = U_START % 2
    assert U_MID % 2 == 0

    def bodies(run, fori):
        run(0, first_body, U0 + units_in(PROLOGUE), 0)
        with fori(1, NB - 1) as b:
            run(b, middle_body, U0 + U_START - U_MID, U_MID)
        run(NB - 1, last_body, U0 + U_START + (NB - 2) * U_MID, 0)

    U_END = U0 + U_START + (NB - 2) * U_MID + units_in(last_body)

    qk_dram = nc.dram_tensor("qk_parts", [2, 3, C, NTOK], BF16, kind="Internal").ap()
    max_dram = nc.dram_tensor("maxima", [NB * NG, 3 * GH * TT, P], BF16, kind="Internal").ap()
    rows_dram = nc.dram_tensor("expert_rows", [NE * REGION + P, ROW], F32, kind="Internal").ap()

    ctx = ExitStack()
    with ctx:
        def sb(name, shape, dt=F32):
            return ctx.enter_context(nc.sbuf_tensor(name, shape, dt))

        def sem(name):
            return ctx.enter_context(nc.semaphore(name))

        wq = sb("wq", [P, CC, C])
        wc = sb("wc", [P, CC, LAT])
        wk = sb("wk", [P, C])
        wv = sb("wv", [P, C])
        wo = sb("wo", [P, CC, C])
        wr = sb("wr", [P, CC, NE])
        bias = sb("bias", [P, C])
        gate = sb("gate", [P, NE, CC, NI])
        up = sb("up", [P, NE, CC, NI])
        down = sb("down", [P, NE, IC, C])
        stacks = down[:, :, :, :].rearrange("p e i c -> p (e i c)").bitcast(BF16)
        q_stack = stacks[:, 0:NH * T].rearrange("p (h t) -> p h t", h=NH)
        k_stack = stacks[:, NH * T:2 * NH * T].rearrange("p (h t) -> p h t", h=NH)
        ident = sb("ident", [P, P])
        ident_b = sb("ident_b", [P, P], BF16)
        causal = sb("causal", [P, P], BF16)
        earlier = sb("earlier", [P, P], BF16)
        ones_b = sb("ones_b", [P, P], BF16)
        expert8 = sb("expert8", [P, NE])
        tile_no = sb("tile_no", [P, NT])
        minus_half = sb("minus_half", [P, TT])
        padding = sb("padding", [P, ROW])
        xt = sb("xt", [P, TT, C])
        xT = sb("xT", [P, CC, T])
        cT = sb("cT", [P, T])
        parts = [[sb(f"part{i}{s}", [P, CC, T], BF16) for s in range(3)] for i in range(2)]
        rest = sb("rest", [P, CC, T])
        vv = sb("vv", [P, TT, NH * VW + HS - 1])
        row_max = sb("row_max", [P, GH, TT])
        max_parts = sb("max_parts", [P, 3, GH, TT], BF16)
        max_rest = sb("max_rest", [P, GH, TT])
        maxT = sb("maxT", [3 * GH * TT, P], BF16)
        probs = sb("probs", [P, BANKS, T])
        oT = sb("oT", [P, 2, T])
        rsum = sb("rsum", [P, TT, GH])
        y = sb("y", [P, TT, C])
        yT = sb("yT", [P, CC, T])
        xr = sb("xr", [P, TT, ROW])
        stats = sb("stats", [P, TT, 6])
        mean_var = sb("mean_var", [P, TT, 2])
        rstd = sb("rstd", [P, TT])
        x1T = sb("x1T", [P, CC, T])
        route = sb("route", [P, TT, NE])
        pick = sb("pick", [P, TT, NE])
        pick_min = sb("pick_min", [P, TT])
        onehot = sb("onehot", [P, TT, NE], BF16)
        next_row = sb("next_row", [P, NE])
        region0 = sb("region0", [P, NE])
        place = sb("place", [P, TT, NE])
        dest = sb("dest", [P, TT])
        dest_i = sb("dest_i", [P, TT], I32)
        token_no = sb("token_no", [P, TT])
        t8 = sb("t8", [P, 4, NE])
        t8i = sb("t8i", [P, NE], I32)
        one8 = sb("one8", [P, NE])
        sel = sb("sel", [P, 2, NT, NE])
        tab = sb("tab", [P, 4, NT])
        row_tab = sb("row_tab", [P, NT], I32)
        expert_tab = sb("expert_tab", [P, NT], I32)
        pad_tab = sb("pad_tab", [P, NE], I32)
        xs = sb("xs", [P, 2, ROW])
        xsT = sb("xsT", [P, 2, CC * P])
        silu = sb("silu", [P, 2, NI])
        hh = sb("hh", [P, 2, NI])
        hT = sb("hT", [P, 2, NI])
        z = sb("z", [P, 2, C])
        zstats = sb("zstats", [P, 2, 6])
        zmv = sb("zmv", [P, 2, 2])
        zrstd = sb("zrstd", [P, 2])
        zi = sb("zi", [P, 2], I32)

        pa = ctx.enter_context(nc.psum_tensor("pa", [P, 2, 2, T], F32))
        pb = ctx.enter_context(nc.psum_tensor("pb", [P, 2, T], F32))
        pv = ctx.enter_context(nc.psum_tensor("pv", [P, 2, T], F32))

        const_done = sem("const_done")
        ones_done = sem("ones_done")
        weights_in = sem("weights_in")
        gate_up_in = sem("gate_up_in")
        down_in = sem("down_in")
        xt_in = sem("xt_in")
        xr_in = sem("xr_in")
        unit_ready = sem("unit_ready")
        unit_read = [sem("unit0_read"), sem("unit1_read")]
        high_ready = sem("high_ready")
        mid_ready = sem("mid_ready")
        low_ready = sem("low_ready")
        parts_out = sem("parts_out")
        stack_in = [sem(f"stack_in{g}") for g in range(NG)]
        max_parts_ready = sem("max_parts_ready")
        max_out = sem("max_out")
        max_in = [sem("max_in0"), sem("max_in1")]
        scores_ready = sem("scores_ready")
        exp_done = sem("exp_done")
        masked = sem("masked")
        pv_done = sem("pv_done")
        oT_ready = sem("oT_ready")
        xr_biased = sem("xr_biased")
        var_ready = sem("var_ready")
        rstd_ready = sem("rstd_ready")
        x1_ready = sem("x1_ready")
        onehot_ready = sem("onehot_ready")
        dest_ready = sem("dest_ready")
        scattered = sem("scattered")
        tables_ready = sem("tables_ready")
        pads_out = sem("pads_out")
        dve_chain = sem("dve_chain")
        pool_chain = sem("pool_chain")
        xs_in = [sem("xs_in0"), sem("xs_in1")]
        xsT_psum = sem("xsT_psum")
        xsT_ready = sem("xsT_ready")
        gate_ready = sem("gate_ready")
        up_ready = sem("up_ready")
        silu_done = sem("silu_done")
        h_ready = sem("h_ready")
        hT_psum = sem("hT_psum")
        hT_ready = sem("hT_ready")
        y2_ready = sem("y2_ready")
        z_ready = sem("z_ready")
        zvar_ready = sem("zvar_ready")
        zrstd_ready = sem("zrstd_ready")
        zstats_ready = sem("zstats_ready")
        zeps_ready = sem("zeps_ready")
        z_normed = sem("z_normed")
        out_done = [sem("out_done0"), sem("out_done1")]

        def slot(idx):
            return idx % 2

        def wait_read(engine, n, b, per):
            earlier_ones = n // 2 - (U0 if n % 2 == 0 else 0)
            engine.wait_ge(unit_read[n % 2], earlier_ones + 1 + b * (per // 2))

        def wait_banks(pe, n, b, per):
            earlier_ones = n // 2 - (U0 if n % 2 == 0 else 0)
            wait(pe, unit_read[n % 2], earlier_ones + b * (per // 2))

        def apart(engine):
            engine.nop(nofuse=True)

        block = ctx.enter_context(nc.Block())

        @block.sync
        def _(sp):
            sp.dma_start(xt[:], tokens[:, 0:TT, :]).then_inc(xt_in, 16)
            sp.dma_start(wq[:], Wq.rearrange("(k p) n -> p k n", p=P)).then_inc(weights_in, 16)
            sp.dma_start(wc[:], Wc.rearrange("(k p) n -> p k n", p=P)).then_inc(weights_in, 16)
            sp.dma_start(wk[:], Wk).then_inc(weights_in, 16)
            sp.dma_start(wv[:], Wv).then_inc(weights_in, 16)
            sp.dma_start(wo[:], Wo.rearrange("(k p) n -> p k n", p=P)).then_inc(weights_in, 16)
            sp.dma_start(wr[:], router_w.rearrange("(k p) n -> p k n", p=P)).then_inc(weights_in, 16)
            sp.dma_start(bias[:], bo.rearrange("(o n) -> o n", o=1).to_broadcast([P, C])).then_inc(weights_in, 16)

            def spill_parts(bn):
                for i in range(2):
                    for s, made in ((0, high_ready), (1, mid_ready), (2, low_ready)):
                        sp.wait_ge(made, bn * 2 + i + 1)
                        dst = qk_dram[i, s].rearrange("(k p) t -> p k t", p=P)
                        sp.dma_start(dst[:, :, bass.ds(bn * T, T)], parts[i][s][:]).then_inc(parts_out, 16)

            def load_stacks(bn, g):
                for i, (stack, which) in enumerate(((q_stack, Q_PART), (k_stack, K_PART))):
                    for r in range(TERMS):
                        src = qk_dram[i, which[r], g * GH * HS:(g + 1) * GH * HS, bass.ds(bn * T, T)]
                        sp.dma_start(stack[r * HS:(r + 1) * HS, g * GH:(g + 1) * GH, :],
                                     src.rearrange("(h d) t -> d h t", d=HS)).then_inc(stack_in[g], 16)

            def move_maxima(b, g, unit, per):
                G = b * NG + g
                wait_read(sp, unit, b, per)
                sp.dma_start(max_dram[bass.ds(G, 1)].rearrange("o r p -> (o r) p"), maxT[:]).then_inc(max_out, 16)
                sp.wait_ge(max_out, G * 16 + 16)
                g4 = g % NG
                src = max_dram[bass.ds(G, 1)].rearrange("o (s r) p -> (o s) (r p)", s=3)
                dst = q_stack[KS:KM, g4 * GH:(g4 + 1) * GH, :].rearrange("s h t -> s (h t)")
                sp.dma_start(dst, src).then_inc(max_in[g % 2], 16)

            def load_residual(b):
                wait(sp, scattered, b * 64)
                sp.dma_start(xr[:, :, 0:C], tokens[:, bass.ds(b * TT, TT), :]).then_inc(xr_in, 16)

            spill_parts(0)
            sp.wait_ge(parts_out, 96)
            for g in range(NG):
                load_stacks(0, g)
            move_maxima(0, 0, unit_numbers(PROLOGUE, "M", U0)[0], 0)
            sp.dma_start(gate[:], gate_w.rearrange("e (k p) n -> p e k n", p=P)).then_inc(gate_up_in, 16)
            sp.dma_start(up[:], up_w.rearrange("e (k p) n -> p e k n", p=P)).then_inc(gate_up_in, 16)

            def run(b, order, const, per):
                first, last = (isinstance(b, int) and b == k for k in (0, NB - 1))
                if not last:
                    sp.wait_ge(high_ready, b * 2 + 1)
                    sp.dma_start(xt[:], tokens[:, bass.ds((b + 1) * TT, TT), :]).then_inc(xt_in, 16)
                if not first:
                    load_residual(b - 1)
                for g in range(NG):
                    if not (last and g == NG - 1):
                        move_maxima(b, g + 1, unit_numbers(order, "M", const)[g], per)
                    if not last:
                        if g == 0:
                            spill_parts(b + 1)
                            sp.wait_ge(parts_out, (b + 1) * 96 + 96)
                        sp.wait_ge(scores_ready, b * NG * BANKS + (g + 1) * BANKS)
                        load_stacks(b + 1, g)

            bodies(run, sp.Fori)
            load_residual(NB - 1)
            sp.wait_ge(scores_ready, NB * NG * BANKS)
            sp.dma_start(down[:], down_w.rearrange("e (k p) n -> p e k n", p=P)).then_inc(down_in, 16)

            sp.wait_ge(tables_ready, 1)
            for e in range(NE):
                row = sp.value_load(pad_tab[0:1, e:e + 1], min_val=e * REGION, max_val=(e + 1) * REGION - P)
                sp.dma_start(rows_dram[bass.ds(row, P), :], padding[:]).then_inc(pads_out, 16)
            sp.dma_start(rows_dram[PAD_ROW:PAD_ROW + P, :], padding[:]).then_inc(pads_out, 16)
            sp.wait_ge(pads_out, (NE + 1) * 16)
            sp.wait_ge(scattered, NB * 64)

            def load_tile(pair, odd):
                i = 2 * pair + odd
                wait(sp, z_normed, i - 1)
                row = sp.value_load(row_tab[0:1, bass.ds(i, 1)], min_val=0, max_val=PAD_ROW)
                sp.dma_start(xs[:, odd, :], rows_dram[bass.ds(row, P), :]).then_inc(xs_in[odd], 16)

            load_tile(0, 0)
            load_tile(0, 1)
            with sp.Fori(1, PAIRS) as p:
                load_tile(p, 0)
                load_tile(p, 1)
            load_tile(PAIRS, 0)
            sp.wait_ge(out_done[0], (NT + 1) // 2 * 16)
            sp.wait_ge(out_done[1], NT // 2 * 16)

        @block.tensor
        def _(pe):
            pe.wait_ge(const_done, 1)
            pe.wait_ge(weights_in, 7 * 16)

            def run(b, order, const, per):
                n, unit = const, {}
                for name, g, u in order:
                    G = b * NG + g
                    s = slot(n)
                    if name in UNITS:
                        wait_banks(pe, n, b, per)
                        unit[name] = n
                        n += 1
                    if name == "X":
                        pe.wait_ge(xt_in, projected(b, g) * 16 + 16)
                        for t in range(TT):
                            for c in range(CC):
                                last = nc.tensor.transpose(pa[:, s, c, t * P:(t + 1) * P],
                                                           xt[:, t, c * P:(c + 1) * P], ident[:])
                    elif name == "Q":
                        wait_read(pe, unit["X"], b, per)
                        for m in range(CC):
                            for c in range(CC):
                                last = nc.tensor.matmul(pa[:, s, m, :], wq[:, c, m * P:(m + 1) * P], xT[:, c, :],
                                                        start=(c == 0), stop=(c == CC - 1))
                    elif name == "C":
                        for c in range(CC):
                            last = nc.tensor.matmul(pa[:, s, 0, :], wc[:, c, :], xT[:, c, :],
                                                    start=(c == 0), stop=(c == CC - 1))
                    elif name == "K":
                        wait_read(pe, unit["C"], b, per)
                        for m in range(CC):
                            last = nc.tensor.matmul(pa[:, s, m, :], wk[:, m * P:(m + 1) * P], cT[:],
                                                    start=True, stop=True)
                    elif name == "V":
                        for t in range(TT):
                            last = nc.tensor.matmul(pa[:, s, t // 2, t % 2 * C:(t % 2 + 1) * C],
                                                    cT[:, t * P:(t + 1) * P], wv[:], start=True, stop=True)
                    elif name == "S":
                        g4 = (g + 2) % NG
                        if u == 0:
                            bs = b if g + 2 < NG else b + 1
                            pe.wait_ge(stack_in[g4], (bs + 1) * 2 * TERMS * 16)

                        def scores(dst, h, qt):
                            hh_ = g4 * GH + h
                            w = (qt + 1) * P
                            nc.tensor.matmul(dst[:, 0:w], q_stack[0:KS, hh_, qt * P:w], k_stack[0:KS, hh_, 0:w],
                                             start=True, stop=False)
                            return nc.tensor.matmul(dst[:, qt * P:w], ident_b[:], causal[:], start=False, stop=True)

                        if u == 0:
                            for h in range(GH):
                                last = scores(pa[:, s, h // 2, h % 2 * 2 * P:(h % 2 + 1) * 2 * P], h, 1)
                        elif u < 3:
                            for j in range(2):
                                scores(pa[:, s, j, 0:3 * P], 2 * (u - 1) + j, 2)
                                last = scores(pa[:, s, j, 3 * P:T], 2 * (u - 1) + j, 0)
                        else:
                            for j in range(2):
                                last = scores(pa[:, s, j, :], 2 * (u - 3) + j, 3)
                    elif name == "M":
                        pe.wait_ge(max_parts_ready, G + 2)
                        apart(pe)
                        last = nc.tensor.transpose(pa[0:3 * GH * TT, s, 0, 0:P // 2].bitcast(BF16),
                                                   max_parts[:, :, :, :].rearrange("p s h t -> p (s h t)"), ident_b[:])
                    elif name == "B":
                        if u == 0:
                            pe.wait_ge(max_in[g % 2], b * 32 + g // 2 * 16 + 16)
                        wait(pe, exp_done, G * BANKS + u - 1)

                        def turned(h, kt, col):
                            hh_ = g * GH + h
                            w = T - kt * P
                            return nc.tensor.matmul(pb[:, u % 2, col:col + w], k_stack[0:KM, hh_, kt * P:(kt + 1) * P],
                                                    q_stack[0:KM, hh_, kt * P:T], start=True, stop=True)

                        if u < 4:
                            last = turned(u, 0, 0)
                        elif u < 8:
                            turned(u - 4, 1, 0)
                            last = turned(u - 4, 3, 3 * P)
                        else:
                            for j in range(2):
                                last = turned(2 * (u - 8) + j, 2, j * 2 * P)
                        last.then_inc(scores_ready, 1)
                    elif name == "PV":
                        if u == 2:
                            G = G - 1
                        bank = (g - (u == 2)) % 2
                        g4 = (g - (u == 2)) % NG
                        if u == 0:
                            wait(pe, oT_ready, G - 1)
                        if u == 0 and g == 0:
                            wait_read(pe, unit["V"], b, per)
                        pe.wait_ge(masked, G * 3 + u + 1)
                        for kt in ((0,), (1, 3), (2,))[u]:
                            for h in range(GH):
                                hh_ = g4 * GH + h
                                if kt == 0:
                                    moving = probs[:, h, :]
                                elif kt == 2:
                                    moving = probs[:, 8 + h // 2, h % 2 * 2 * P:(h % 2 + 1) * 2 * P]
                                else:
                                    moving = probs[:, 4 + h, 0:3 * P] if kt == 1 else probs[:, 4 + h, 3 * P:T]
                                last = nc.tensor.matmul(pv[32 * h:32 * h + 32, bank, kt * P:T],
                                                        vv[:, kt, hh_ * VW:hh_ * VW + 32], moving,
                                                        start=(kt == 0), stop=(kt == 2))
                        last.then_inc(pv_done, 1)
                    elif name == "OT":
                        pe.wait_ge(oT_ready, G)
                        for t in range(TT):
                            last = nc.tensor.transpose(pa[:, s, 0, t * P:(t + 1) * P],
                                                       oT[:, (g - 1) % 2, t * P:(t + 1) * P], ident[:])
                    elif name == "YT":
                        wait_read(pe, unit["OT"], b, per)
                        for t in range(TT):
                            for c in range(CC):
                                last = nc.tensor.transpose(pa[:, s, c, t * P:(t + 1) * P],
                                                           y[:, t, c * P:(c + 1) * P], ident[:])
                    elif name == "WO":
                        wait_read(pe, unit["YT"], b, per)
                        for t in range(TT):
                            for c in range(CC):
                                last = nc.tensor.matmul(pa[:, s, t // 2, t % 2 * C:(t % 2 + 1) * C],
                                                        yT[:, c, t * P:(t + 1) * P], wo[:, c, :],
                                                        start=(c == 0), stop=(c == CC - 1))
                    elif name == "X1T":
                        pe.wait_ge(x1_ready, past(b, g))
                        for t in range(TT):
                            for c in range(CC):
                                last = nc.tensor.transpose(pa[:, s, c, t * P:(t + 1) * P],
                                                           xr[:, t, c * P:(c + 1) * P], ident[:])
                    elif name == "R":
                        wait_read(pe, unit["X1T"], b, per)
                        for t in range(TT):
                            for c in range(CC):
                                last = nc.tensor.matmul(pa[:, s, 0, t * NE:(t + 1) * NE],
                                                        x1T[:, c, t * P:(t + 1) * P], wr[:, c, :],
                                                        start=(c == 0), stop=(c == CC - 1))
                    elif name == "RK":
                        pe.wait_ge(onehot_ready, past(b, g))
                        for t in range(TT + 1):
                            dst = pa[:, s, 0, t * NE:(t + 1) * NE]
                            for t2 in range(min(t, TT)):
                                last = nc.tensor.matmul(dst, ones_b[:], onehot[:, t2, :], start=(t2 == 0),
                                                        stop=(t == TT and t2 == TT - 1))
                            if t < TT:
                                last = nc.tensor.matmul(dst, earlier[:], onehot[:, t, :], start=(t == 0), stop=True)
                    if name in UNITS:
                        last.then_inc(unit_ready, 1)

            run(0, PROLOGUE, U0, 0)
            bodies(run, pe.Fori)
            run(NB - 1, EPILOGUE, U_END, 0)

            pe.wait_ge(gate_up_in, 32)
            pe.wait_ge(tables_ready, 1)

            def gate_up(pair, odd):
                i = 2 * pair + odd
                expert = pe.value_load(expert_tab[0:1, bass.ds(i, 1)], min_val=0, max_val=NE - 1)
                pe.wait_ge(xs_in[odd], pair * 16 + 16)
                wait(pe, xsT_ready, i)
                for c in range(CC):
                    last = nc.tensor.transpose(pv[:, 0, c * P:(c + 1) * P], xs[:, odd, c * P:(c + 1) * P], ident[:])
                last.then_inc(xsT_psum, 1)
                pe.wait_ge(xsT_ready, i + 1)
                wait(pe, silu_done, i - 1)
                for c in range(CC):
                    last = nc.tensor.matmul(pa[:, odd, 0, :], xsT[:, odd, c * P:(c + 1) * P],
                                            gate[:, bass.ds(expert, 1), c, :].rearrange("p o n -> p (o n)"), start=(c == 0), stop=(c == CC - 1))
                last.then_inc(gate_ready, 1)
                wait(pe, h_ready, i - 1)
                for c in range(CC):
                    last = nc.tensor.matmul(pa[:, odd, 1, :], xsT[:, odd, c * P:(c + 1) * P],
                                            up[:, bass.ds(expert, 1), c, :].rearrange("p o n -> p (o n)"), start=(c == 0), stop=(c == CC - 1))
                last.then_inc(up_ready, 1)

            def down_of(pair, odd):
                i = 2 * pair + odd
                expert = pe.value_load(expert_tab[0:1, bass.ds(i, 1)], min_val=0, max_val=NE - 1)
                pe.wait_ge(h_ready, i + 1)
                wait(pe, hT_ready, i)
                for c in range(IC):
                    last = nc.tensor.transpose(pb[:, 0, c * P:(c + 1) * P], hh[:, odd, c * P:(c + 1) * P], ident[:])
                last.then_inc(hT_psum, 1)
                pe.wait_ge(hT_ready, i + 1)
                wait(pe, z_ready, i)
                for c in range(IC):
                    last = nc.tensor.matmul(pb[:, 1, 0:C], hT[:, odd, c * P:(c + 1) * P],
                                            down[:, bass.ds(expert, 1), c, :].rearrange("p o n -> p (o n)"), start=(c == 0), stop=(c == IC - 1))
                last.then_inc(y2_ready, 1)

            gate_up(0, 0)
            gate_up(0, 1)
            pe.wait_ge(down_in, 16)
            down_of(0, 0)
            with pe.Fori(1, PAIRS) as p:
                gate_up(p, 0)
                down_of(p - 1, 1)
                gate_up(p, 1)
                down_of(p, 0)
            gate_up(PAIRS, 0)
            down_of(PAIRS - 1, 1)
            down_of(PAIRS, 0)

        @block.scalar
        def _(act):
            nc.scalar.preload_act_table(ACT.Exp)
            act.wait_ge(ones_done, 1)

            def run(b, order, const, per):
                n = const
                for name, g, u in order:
                    G = b * NG + g
                    s = slot(n)
                    n += name in UNITS
                    ready = n - U0 + b * per
                    if name == "X":
                        act.wait_ge(unit_ready, ready)
                        nc.scalar.activation(xT[:], pa[:, s, :, :], ACT.Copy)\
                            .then_inc(unit_read[s], 1)
                    elif name in ("Q", "K"):
                        i = int(name == "K")
                        act.wait_ge(unit_ready, ready)
                        wait(act, parts_out, projected(b, g) * 96)
                        nc.scalar.activation(parts[i][0][:], pa[:, s, :, :], ACT.Copy).then_inc(high_ready, 1)
                    elif name == "C":
                        act.wait_ge(unit_ready, ready)
                        nc.scalar.activation(cT[:], pa[:, s, 0, :], ACT.Copy)\
                            .then_inc(unit_read[s], 1)
                    elif name == "V":
                        act.wait_ge(unit_ready, ready)
                        v4 = vv[:, :, 0:NH * VW].rearrange("p t (h d) -> p t h d", d=VW)
                        for t in range(TT):
                            last = nc.scalar.activation(v4[:, t, :, 0:HS],
                                                        pa[:, s, t // 2, t % 2 * C:(t % 2 + 1) * C]
                                                        .rearrange("p (h d) -> p h d", d=HS), ACT.Copy)
                        last.then_inc(unit_read[s], 1)
                    elif name == "B":
                        act.wait_ge(scores_ready, G * BANKS + u + 1)
                        wait(act, pv_done, (G - 1) * 3 + (1 if u < 4 else 2 if u < 8 else 3))
                        nc.scalar.activation(probs[:, u, :], pb[:, u % 2, :], ACT.Exp, scale=SCORE_SCALE)\
                            .then_inc(exp_done, 1)
                    elif name == "PV" and u == 2:
                        act.wait_ge(pv_done, G * 3)
                        nc.scalar.activation(oT[:, (g - 1) % 2, :], pv[:, (g - 1) % 2, :], ACT.Copy)\
                            .then_inc(oT_ready, 1)
                    elif name == "YT":
                        act.wait_ge(unit_ready, ready)
                        nc.scalar.activation(yT[:], pa[:, s, :, :], ACT.Copy)\
                            .then_inc(unit_read[s], 1)
                    elif name == "X1T":
                        act.wait_ge(unit_ready, ready)
                        nc.scalar.activation(x1T[:], pa[:, s, :, :], ACT.Copy)\
                            .then_inc(unit_read[s], 1)
                    elif name == "R":
                        act.wait_ge(unit_ready, ready)
                        nc.scalar.activation(route[:, :, :].rearrange("p t e -> p (t e)"), pa[:, s, 0, 0:TT * NE],
                                             ACT.Exp, scale=-1.0)\
                            .then_inc(unit_read[s], 1)

            run(0, PROLOGUE, U0, 0)
            bodies(run, act.Fori)
            run(NB - 1, EPILOGUE, U_END, 0)

            def rows_turned(pair, odd):
                i = 2 * pair + odd
                act.wait_ge(xsT_psum, i + 1)
                nc.scalar.activation(xsT[:, odd, :], pv[:, 0, 0:CC * P], ACT.Copy).then_inc(xsT_ready, 1)

            def inner(pair, odd):
                i = 2 * pair + odd
                act.wait_ge(gate_ready, i + 1)
                wait(act, h_ready, i - 1)
                nc.scalar.activation(silu[:, odd, :], pa[:, odd, 0, :], ACT.Silu).then_inc(silu_done, 1)

            def inner_turned(pair, odd):
                i = 2 * pair + odd
                act.wait_ge(hT_psum, i + 1)
                nc.scalar.activation(hT[:, odd, :], pb[:, 0, :], ACT.Copy).then_inc(hT_ready, 1)

            nc.scalar.preload_act_table(ACT.Silu)
            rows_turned(0, 0)
            inner(0, 0)
            rows_turned(0, 1)
            inner(0, 1)
            inner_turned(0, 0)
            with act.Fori(1, PAIRS) as p:
                rows_turned(p, 0)
                inner(p, 0)
                inner_turned(p - 1, 1)
                rows_turned(p, 1)
                inner(p, 1)
                inner_turned(p, 0)
            rows_turned(PAIRS, 0)
            inner(PAIRS, 0)
            inner_turned(PAIRS - 1, 1)
            inner_turned(PAIRS, 0)

        @block.vector
        def _(dve):
            chain = Chain(dve, dve_chain, DVE_LINKS)
            V = nc.vector

            def run(b, order, const, per):
                n = const
                for name, g, u in order:
                    G = b * NG + g
                    s = slot(n)
                    n += name in UNITS
                    ready = n - U0 + b * per
                    if name in ("Q", "K"):
                        i = int(name == "K")
                        two = projected(b, g) * 2 + i
                        dve.wait_ge(high_ready, two + 1)
                        wait(dve, low_ready, two)
                        V.tensor_tensor(rest[:], pa[:, s, :, :], parts[i][0][:], ALU.subtract).then_inc(unit_read[s], 1)
                        wait_read(dve, n - 1, b, per)
                        V.tensor_copy(parts[i][1][:], rest[:]).then_inc(mid_ready, 1)
                    elif name == "S":
                        dve.wait_ge(unit_ready, ready)
                        if u == 0:
                            V.tensor_reduce(row_max[:, :, 1], pa[:, s, :, :].rearrange("p k (h t) -> p (k h) t", h=2),
                                            AX.X, ALU.max).then_inc(unit_read[s], 1)
                        elif u < 3:
                            h = 2 * (u - 1)
                            V.tensor_reduce(row_max[:, h:h + 2, 2], pa[:, s, :, 0:3 * P], AX.X, ALU.max)
                            V.tensor_reduce(row_max[:, h:h + 2, 0], pa[:, s, :, 3 * P:T], AX.X, ALU.max)\
                                .then_inc(unit_read[s], 1)
                        else:
                            h = 2 * (u - 3)
                            last = V.tensor_reduce(row_max[:, h:h + 2, 3], pa[:, s, :, :], AX.X, ALU.max)
                            last.then_inc(unit_read[s], 1)
                        if u == 4:
                            wait_read(dve, n - 1, b, per)
                            high, mid, low = (max_parts[:, i, :, :] for i in range(3))
                            chain.link(V.tensor_scalar(high, row_max[:], -1.0, None, ALU.mult))
                            chain.link(V.scalar_tensor_tensor(max_rest[:], row_max[:], -1.0, high, ALU.mult, ALU.subtract))
                            chain.link(V.tensor_copy(mid, max_rest[:]))
                            V.tensor_tensor(low, max_rest[:], mid, ALU.subtract).then_inc(max_parts_ready, 1)
                    elif name == "M":
                        dve.wait_ge(unit_ready, ready)
                        wait(dve, max_out, (G + 1) * 16)
                        V.tensor_copy(maxT[:], pa[0:3 * GH * TT, s, 0, 0:P // 2].bitcast(BF16))\
                            .then_inc(unit_read[s], 1)
                    elif name == "OT":
                        dve.wait_ge(unit_ready, ready)
                        o4 = pa[:, s, 0, :].rearrange("p (t h d) -> p t h d", t=TT, h=GH)
                        chain.link(V.reciprocal(rsum[:], o4[:, :, :, HS]))
                        ch = (g - 1) % NG * GH * HS
                        y4 = y[:, :, ch:ch + GH * HS].rearrange("p t (h d) -> p t h d", h=GH)
                        V.tensor_tensor(y4, o4[:, :, :, 0:HS],
                                        rsum[:, :, :].rearrange("p t (h o) -> p t h o", o=1).to_broadcast([P, TT, GH, HS]),
                                        ALU.mult).then_inc(unit_read[s], 1)
                    elif name == "WO":
                        dve.wait_ge(unit_ready, ready)
                        dve.wait_ge(xr_biased, past(b, g))
                        last = V.tensor_tensor(xr[:, :, 0:C], pa[:, s, :, :].rearrange("p k (t c) -> p (k t) c", t=2),
                                               xr[:, :, 0:C], ALU.add)
                        last.then_inc(unit_read[s], 1)
                        wait_read(dve, n - 1, b, per)
                        for t in range(TT):
                            last = V.bn_stats(stats[:, t, :], xr[:, t, 0:C])
                        chain.link(last)
                        apart(dve)
                        for t in range(TT):
                            last = V.bn_aggr(mean_var[:, t, :], stats[:, t, :])
                        last.then_inc(var_ready, 1)
                    elif name == "LN":
                        dve.wait_ge(rstd_ready, past(b, g))
                        for t in range(TT):
                            last = V.tensor_scalar(xr[:, t, 0:C], xr[:, t, 0:C], mean_var[:, t, 0:1], rstd[:, t:t + 1],
                                                   ALU.subtract, ALU.mult)
                        last.then_inc(x1_ready, 1)
                    elif name == "R":
                        wait_read(dve, n - 1, b, per)
                        chain.link(V.tensor_scalar(route[:], route[:], 1.0, None, ALU.add))
                        chain.link(V.reciprocal(route[:], route[:]))
                        chain.link(V.tensor_reduce(xr[:, :, C], route[:], AX.X, ALU.max))
                        chain.link(V.tensor_tensor(pick[:], route[:],
                                                   xr[:, :, C:C + 1].to_broadcast([P, TT, NE]), ALU.is_equal))
                        e8 = expert8[:, :].rearrange("p (o e) -> p o e", o=1).to_broadcast([P, TT, NE])
                        chain.link(V.tensor_tensor(pick[:], pick[:], e8, ALU.mult))
                        chain.link(V.tensor_reduce(pick_min[:], pick[:], AX.X, ALU.min))
                        V.tensor_tensor(onehot[:], e8, pick_min[:, :].rearrange("p (t o) -> p t o", o=1)
                                        .to_broadcast([P, TT, NE]), ALU.is_equal).then_inc(onehot_ready, 1)
                    elif name == "RK":
                        dve.wait_ge(unit_ready, ready)
                        ranks = pa[:, s, 0, 0:(TT + 1) * NE].rearrange("p (t e) -> p t e", e=NE)
                        nr = next_row[:, :].rearrange("p (o e) -> p o e", o=1)
                        chain.link(V.tensor_tensor(place[:], ranks[:, 0:TT, :], nr.to_broadcast([P, TT, NE]), ALU.add))
                        chain.link(V.tensor_tensor(place[:], place[:], onehot[:], ALU.mult))
                        V.tensor_tensor(nr, ranks[:, TT:TT + 1, :], nr, ALU.add).then_inc(unit_read[s], 1)
                        chain.link(V.tensor_reduce(dest[:], place[:], AX.X, ALU.add))
                        chain.link(V.tensor_copy(xr[:, :, C + 1], token_no[:]))
                        chain.link(V.tensor_scalar(token_no[:], token_no[:], float(T), None, ALU.add))
                        V.tensor_copy(dest_i[:], dest[:]).then_inc(dest_ready, 1)

            V.memset(vv[:], 1.0)
            V.memset(k_stack[KS:KM, :, :], 1.0)
            V.memset(padding[:, 0:C + 1], 0.0)
            V.memset(padding[:, C + 1:ROW], NO_TOKEN)
            V.memset(minus_half[:], -0.5)
            V.memset(one8[:], 1.0).then_inc(ones_done, 1)
            dve.wait_ge(ones_done, 1)
            dve.wait_ge(const_done, 1)
            chain.link(V.tensor_scalar(region0[:], expert8[:], float(NE), float(REGION), ALU.add, ALU.mult))
            chain.link(V.tensor_copy(next_row[:], region0[:]))

            run(0, PROLOGUE, U0, 0)
            bodies(chain.counted(run), dve.Fori)
            run(NB - 1, EPILOGUE, U_END, 0)

            rows, tiles, upto, before = (t8[:, k, :] for k in range(4))
            chain.link(V.tensor_copy(pad_tab[:], next_row[:]))
            chain.link(V.tensor_tensor(rows, next_row[:], region0[:], ALU.subtract))
            chain.link(V.tensor_scalar(rows, rows, float(P - 1), None, ALU.add))
            chain.link(V.tensor_copy(t8i[:], rows))
            chain.link(V.tensor_single_scalar(t8i[:], t8i[:], 7, ALU.arith_shift_right))
            chain.link(V.tensor_copy(tiles, t8i[:]))
            chain.link(V.tensor_tensor_scan(upto, one8[:], tiles, 0.0, ALU.mult, ALU.add))
            chain.link(V.tensor_tensor(before, upto, tiles, ALU.subtract))

            def by_tile(a):
                return a.rearrange("p (o e) -> p o e", o=1).to_broadcast([P, NT, NE])

            no = tile_no[:, :].rearrange("p (t o) -> p t o", o=1).to_broadcast([P, NT, NE])
            s0, s1 = sel[:, 0], sel[:, 1]
            chain.link(V.tensor_tensor(s0, no, by_tile(before), ALU.is_ge))
            chain.link(V.tensor_tensor(s1, no, by_tile(upto), ALU.is_lt))
            chain.link(V.tensor_tensor(s0, s0, s1, ALU.mult))
            chain.link(V.scalar_tensor_tensor(before, before, -float(P), region0[:], ALU.mult, ALU.add))
            chain.link(V.tensor_tensor(s1, s0, by_tile(before), ALU.mult))
            base, used, away, number = (tab[:, k, :] for k in range(4))
            chain.link(V.tensor_reduce(base, s1, AX.X, ALU.add))
            chain.link(V.tensor_reduce(used, s0, AX.X, ALU.add))
            chain.link(V.tensor_scalar(away, tile_no[:], float(P), -float(PAD_ROW), ALU.mult, ALU.add))
            chain.link(V.tensor_tensor(away, away, used, ALU.mult))
            chain.link(V.tensor_tensor(base, base, away, ALU.add))
            chain.link(V.tensor_scalar(base, base, float(PAD_ROW), None, ALU.add))
            chain.link(V.tensor_copy(row_tab[:], base))
            chain.link(V.tensor_tensor(s1, s0, by_tile(expert8[:, :]), ALU.mult))
            chain.link(V.tensor_reduce(number, s1, AX.X, ALU.add))
            chain.link(V.tensor_scalar(number, number, float(NE), float(NE - 1), ALU.add, ALU.min))
            V.tensor_copy(expert_tab[:], number).then_inc(tables_ready, 1)

            def inner(pair, odd):
                i = 2 * pair + odd
                dve.wait_ge(silu_done, i + 1)
                dve.wait_ge(up_ready, i + 1)
                wait(dve, hT_psum, i - 1)
                V.tensor_tensor(hh[:, odd, :], pa[:, odd, 1, :], silu[:, odd, :], ALU.mult).then_inc(h_ready, 1)

            def outer(pair, odd):
                i = 2 * pair + odd
                dve.wait_ge(y2_ready, i + 1)
                wait(dve, out_done[odd], pair * 16)
                V.scalar_tensor_tensor(z[:, odd, :], pb[:, 1, 0:C], xs[:, odd, C:C + 1], xs[:, odd, 0:C],
                                       ALU.mult, ALU.add).then_inc(z_ready, 1)
                dve.wait_ge(z_ready, i + 1)
                V.bn_stats(zstats[:, odd, :], z[:, odd, :]).then_inc(zstats_ready, 1)
                V.tensor_copy(zi[:, odd:odd + 1], xs[:, odd, C + 1:C + 2])
                dve.wait_ge(zstats_ready, i + 1)
                apart(dve)
                V.bn_aggr(zmv[:, odd, :], zstats[:, odd, :]).then_inc(zvar_ready, 1)
                dve.wait_ge(zrstd_ready, i + 1)
                V.tensor_scalar(z[:, odd, :], z[:, odd, :], zmv[:, odd, 0:1], zrstd[:, odd:odd + 1],
                                ALU.subtract, ALU.mult).then_inc(z_normed, 1)

            inner(0, 0)
            inner(0, 1)
            outer(0, 0)
            with dve.Fori(1, PAIRS) as p:
                inner(p, 0)
                outer(p - 1, 1)
                inner(p, 1)
                outer(p, 0)
            inner(PAIRS, 0)
            outer(PAIRS - 1, 1)
            outer(PAIRS, 0)

        @block.gpsimd
        def _(pool):
            g_ = nc.gpsimd
            chain = Chain(pool, pool_chain, POOL_LINKS)
            g_.memset(ident[:], 0.0)
            g_.memset(ident_b[:], 0.0)
            g_.memset(causal[:], 0.0)
            g_.memset(earlier[:], 1.0)
            g_.memset(ones_b[:], 1.0)
            g_.iota(expert8[:], [[1, NE]], base=-NE, channel_multiplier=0, allow_small_or_imprecise_dtypes=True)
            g_.iota(tile_no[:], [[1, NT]], base=0, channel_multiplier=0, allow_small_or_imprecise_dtypes=True)
            chain.link(g_.iota(token_no[:], [[P, TT]], base=0, channel_multiplier=1,
                               allow_small_or_imprecise_dtypes=True))
            for m in (ident, ident_b):
                g_.affine_select(out=m[:], in_=m[:], pattern=[[-1, P]], compare_op=ALU.not_equal, fill=1.0,
                                 base=0, channel_multiplier=1)
            g_.affine_select(out=causal[:], in_=causal[:], pattern=[[-1, P]], compare_op=ALU.is_ge, fill=MASKED,
                             base=0, channel_multiplier=1)
            g_.affine_select(out=earlier[:], in_=earlier[:], pattern=[[1, P]], compare_op=ALU.is_gt, fill=0.0,
                             base=0, channel_multiplier=-1).then_inc(const_done, 1)

            def clear_later(view, blocks):
                return g_.affine_select(out=view, in_=view, pattern=[[0, k] for k in blocks] + [[1, P]],
                                        compare_op=ALU.is_ge, fill=0.0, base=0, channel_multiplier=-1)

            def run(b, order, const, per):
                for name, g, u in order:
                    G = b * NG + g
                    if name in ("Q", "K"):
                        i = int(name == "K")
                        pool.wait_ge(mid_ready, projected(b, g) * 2 + i + 1)
                        g_.tensor_tensor(parts[i][2][:], rest[:], parts[i][1][:], ALU.subtract).then_inc(low_ready, 1)
                    elif name == "B" and u in (3, 7, 9):
                        pool.wait_ge(exp_done, G * BANKS + u + 1)
                        apart(pool)
                        if u == 3:
                            last = clear_later(probs[:, 0:4, 0:P], [GH])
                        elif u == 7:
                            view = probs[:, 4:8, :].rearrange("p h (k q) -> p h k q", q=P)
                            clear_later(view[:, :, 0, :], [GH])
                            last = clear_later(view[:, :, 3, :], [GH])
                        else:
                            view = probs[:, 8:10, :].rearrange("p h (k q) -> p (h k) q", q=2 * P)
                            last = clear_later(view[:, :, 0:P], [GH])
                        last.then_inc(masked, 1)
                    elif name == "YT":
                        pool.wait_ge(xr_in, (past(b, g)) * 16)
                        g_.tensor_tensor(xr[:, :, 0:C], xr[:, :, 0:C],
                                         bias[:, :].rearrange("p (o c) -> p o c", o=1).to_broadcast([P, TT, C]),
                                         ALU.add).then_inc(xr_biased, 1)
                    elif name == "LN":
                        pool.wait_ge(var_ready, past(b, g))
                        apart(pool)
                        chain.link(g_.tensor_scalar(rstd[:], mean_var[:, :, 1], EPS, None, ALU.add))
                        g_.tensor_tensor(rstd[:], rstd[:], minus_half[:], ALU.pow).then_inc(rstd_ready, 1)
                    elif name == "RK":
                        pool.wait_ge(dest_ready, past(b, g))
                        apart(pool)
                        for t in range(TT):
                            g_.indirect_dma_start(out=rows_dram, out_offset=bass.IndirectOffsetOnAxis(dest_i[:, t:t + 1], 0),
                                                  in_=xr[:, t, :], in_offset=None).then_inc(scattered, 16)

            pool.wait_ge(weights_in, 7 * 16)
            run(0, PROLOGUE, U0, 0)
            bodies(chain.counted(run), pool.Fori)
            run(NB - 1, EPILOGUE, U_END, 0)

            def finish(pair, odd):
                i = 2 * pair + odd
                pool.wait_ge(zvar_ready, i + 1)
                apart(pool)
                g_.tensor_scalar(zrstd[:, odd:odd + 1], zmv[:, odd, 1:2], EPS, None, ALU.add).then_inc(zeps_ready, 1)
                pool.wait_ge(zeps_ready, i + 1)
                g_.tensor_tensor(zrstd[:, odd:odd + 1], zrstd[:, odd:odd + 1], minus_half[:, 0:1], ALU.pow)\
                    .then_inc(zrstd_ready, 1)
                pool.wait_ge(z_normed, i + 1)
                apart(pool)
                g_.indirect_dma_start(out=out_rows, out_offset=bass.IndirectOffsetOnAxis(zi[:, odd:odd + 1], 0),
                                      in_=z[:, odd, :], in_offset=None, bounds_check=NTOK - 1, oob_is_err=False)\
                    .then_inc(out_done[odd], 16)

            finish(0, 0)
            finish(0, 1)
            with pool.Fori(1, PAIRS) as p:
                finish(p, 0)
                finish(p, 1)
            finish(PAIRS, 0)


_INS = ["L0_attn_x", "L0_attn_Wq", "L0_attn_Wc", "L0_attn_Wk", "L0_attn_Wv", "L0_attn_Wo", "L0_attn_bo",
        "L0_ffn_router_w", "L0_ffn_gate_w", "L0_ffn_up_w", "L0_ffn_down_w"]


def kernel(**inputs):
    import numpy as np
    import concourse.bacc as bacc
    from concourse.bass_utils import run_bass_kernel_spmd

    nc = bacc.Bacc("TRN2", target_bir_lowering=False, num_devices=1)
    arrays, args = {}, []
    for name in _INS:
        a = np.ascontiguousarray(inputs[name])
        arrays[name + "_dram"] = a
        args.append(nc.dram_tensor(name + "_dram", a.shape, mybir.dt.from_np(a.dtype), kind="ExternalInput").ap())
    args.append(nc.dram_tensor("out_dram", (NB, T, C), F32, kind="ExternalOutput").ap())
    kernel_program(nc, *args)
    return run_bass_kernel_spmd(nc, [arrays], core_ids=[0]).results[0]["out_dram"]
```

```python
import concourse.bass as bass
from concourse import mybir
from contextlib import ExitStack

F32 = mybir.dt.float32
BF16 = mybir.dt.bfloat16
I32 = mybir.dt.int32
ALU = mybir.AluOpType
ACT = mybir.ActivationFunctionType
AX = mybir.AxisListType

P = 128
NB, T, C = 4, 512, 256
NH, HS = 16, 16
NTOK = NB * T
TT = T // P
CC = C // P
GH = 4
NG = NH // GH
LAT = 128
NE, NI = 8, 512
IC = NI // P
RUNS = [3, 2, 1]
TERMS = sum(RUNS)
KS = TERMS * HS
KM = KS + 3
VW = HS + 1
SCORE_SCALE = HS ** -0.5
EPS = 1e-5
MASKED = -1e30
NT = NTOK // P + NE - 1
REGION = NTOK + P
PAD_ROW = NE * REGION
ROW = C + 2
NO_TOKEN = 4096.0
PAIRS = NT // 2
BANKS = 10


def steps_of(first, last):
    order = []
    for g in range(NG):
        before = not (first and g == 0)
        ahead = not (last and g >= 2)
        project, finish = g == 0 and not last, not first
        order += [("B", g, 0), ("B", g, 1)]
        order += [("PV", g, 2)] * before + [("V", g, 0)] * (g == 0 and not first)
        order += [("YT", g, 0)] * (g == 1 and finish)
        order += [("S", g, 0)] * ahead + [("B", g, 2), ("B", g, 3)]
        order += [("M", g, 0)] * (not (last and g == NG - 1))
        order += [("RV", g, 0)] * (g == 2 and finish)
        order += [("S", g, 1)] * ahead + [("B", g, 4), ("B", g, 5)]
        order += [("LN", g, 0)] * (g == 2 and finish)
        order += [("OT", g, 0)] * before + [("PV", g, 0)]
        order += [("RK", g, 0), ("SC", g, 0)] * (g == 3 and finish)
        order += [("S", g, 2)] * ahead + [("B", g, 6), ("B", g, 7)]
        order += [("SC", g, 1)] * (g == 3 and finish)
        order += [("S", g, 3)] * ahead
        order += [("X", g, 0), ("Q", g, 0), ("QL", g, 0)] * project
        order += [("X1T", g, 0)] * (g == 2 and finish)
        order += [("B", g, 8), ("B", g, 9)] + [("S", g, 4)] * ahead
        order += [("SC", g, 2), ("SC", g, 3)] * (g == 3 and finish)
        order += [("XB", g, 0)] * (g == 0 and finish)
        order += [("C", g, 0), ("K", g, 0), ("KL", g, 0)] * project
        order += [("WO", g, 0)] * (g == 1 and finish)
        order += [("R", g, 0)] * (g == 2 and finish)
        order += [("PV", g, 1)]
    return order


PROLOGUE = ([(x, -3, 0) for x in ("X", "Q", "QL", "C", "K", "KL", "V")] + [("S", -2, u) for u in range(5)]
            + [("S", -1, 0), ("M", -1, 0)] + [("S", -1, u) for u in range(1, 5)])
EPILOGUE = [(x, NG, 2 * (x == "PV")) 
            for x in ("PV", "OT", "XB", "YT", "WO", "RV", "LN", "X1T", "R", "RK")]
EPILOGUE += [("SC", NG, t) for t in range(TT)]
UNITS = ("X", "Q", "C", "K", "V", "S", "M", "OT", "YT", "WO", "X1T", "R", "RK")


def units_in(order):
    return sum(name in UNITS for name, _, _ in order)


def projected(b, g):
    return b + (g >= 0)


def past(b, g):
    return b + (g == NG)


def unit_numbers(order, wanted, n):
    names = [name for name, _, _ in order if name in UNITS]
    return [n + k for k, name in enumerate(names) if name == wanted]


def wait(engine, sem, value):
    if not isinstance(value, int) or value > 0:
        engine.wait_ge(sem, value)


class Chain:

    def __init__(self, engine, sem, per_body):
        self.engine, self.sem, self.per_body = engine, sem, per_body
        self.done, self.batch = 0, None

    def link(self, instruction):
        self.done += 1
        instruction.then_inc(self.sem, 1)
        more = 0 if self.batch is None else (self.batch - 1) * self.per_body
        self.engine.wait_ge(self.sem, self.done + more)

    def counted(self, run):
        def counted_run(b, order, const, per):
            in_loop = not isinstance(b, int)
            self.batch, began = (b if in_loop else None), self.done
            run(b, order, const, per)
            if in_loop:
                assert self.done - began == self.per_body, self.done - began
                self.done += (NB - 3) * self.per_body
            self.batch = None
        return counted_run


DVE_LINKS, POOL_LINKS = 28, 1


def kernel_program(nc, x, Wq, Wc, Wk, Wv, Wo, bo, router_w, gate_w, up_w, down_w, out):
    tokens = x.rearrange("b (t p) c -> p (b t) c", p=P)
    out_rows = out.rearrange("b t c -> (b t) c")
    first_body, middle_body, last_body = steps_of(True, False), steps_of(False, False), steps_of(False, True)
    U_MID = units_in(middle_body)
    U_START = units_in(PROLOGUE) + units_in(first_body)
    U0 = U_START % 2
    assert U_MID % 2 == 0

    def bodies(run, fori):
        run(0, first_body, U0 + units_in(PROLOGUE), 0)
        with fori(1, NB - 1) as b:
            run(b, middle_body, U0 + U_START - U_MID, U_MID)
        run(NB - 1, last_body, U0 + U_START + (NB - 2) * U_MID, 0)

    U_END = U0 + U_START + (NB - 2) * U_MID + units_in(last_body)

    qk_dram = nc.dram_tensor("qk_parts", [NB, 2, 3, C, T], BF16, kind="Internal").ap()
    max_dram = nc.dram_tensor("maxima", [NB * NG, 3 * GH * TT, P], BF16, kind="Internal").ap()
    rows_dram = nc.dram_tensor("expert_rows", [NE * REGION + P, ROW], F32, kind="Internal").ap()

    ctx = ExitStack()
    with ctx:
        def sb(name, shape, dt=F32):
            return ctx.enter_context(nc.sbuf_tensor(name, shape, dt))

        def sem(name):
            return ctx.enter_context(nc.semaphore(name))

        wq = sb("wq", [P, CC, C])
        wc = sb("wc", [P, CC, LAT])
        wk = sb("wk", [P, C])
        wv = sb("wv", [P, C])
        wo = sb("wo", [P, CC, C])
        wr = sb("wr", [P, CC, NE])
        bias = sb("bias", [P, C])
        gate = sb("gate", [P, NE, CC, NI])
        up = sb("up", [P, NE, CC, NI])
        down = sb("down", [P, NE, IC, C])
        stacks = down[:, :, :, :].rearrange("p e i c -> p (e i c)").bitcast(BF16)
        q_stack = stacks[:, 0:NH * T].rearrange("p (h t) -> p h t", h=NH)
        k_stack = stacks[:, NH * T:2 * NH * T].rearrange("p (h t) -> p h t", h=NH)
        ident = sb("ident", [P, P])
        ident_b = sb("ident_b", [P, P], BF16)
        causal = sb("causal", [P, P], BF16)
        earlier = sb("earlier", [P, P], BF16)
        ones_b = sb("ones_b", [P, P], BF16)
        expert8 = sb("expert8", [P, NE])
        tile_no = sb("tile_no", [P, NT])
        minus_half = sb("minus_half", [P, TT])
        padding = sb("padding", [P, ROW])
        xt = sb("xt", [P, TT, C])
        xT = sb("xT", [P, CC, T])
        cT = sb("cT", [P, T])
        parts = [[sb(f"part{i}{s}", [P, CC, T], BF16) for s in range(3)] for i in range(2)]
        rest = sb("rest", [P, CC, T])
        vv = sb("vv", [P, TT, NH * VW + HS - 1])
        row_max = sb("row_max", [P, GH, TT])
        max_parts = sb("max_parts", [P, 3, GH, TT], BF16)
        max_rest = sb("max_rest", [P, GH, TT])
        maxT = sb("maxT", [3 * GH * TT, P], BF16)
        probs = sb("probs", [P, BANKS, T])
        oT = sb("oT", [P, 2, T])
        rsum = sb("rsum", [P, TT, GH])
        y = sb("y", [P, TT, C])
        yT = sb("yT", [P, CC, T])
        xr = sb("xr", [P, TT, ROW])
        stats = sb("stats", [P, TT, 6])
        mean_var = sb("mean_var", [P, TT, 2])
        rstd = sb("rstd", [P, TT])
        x1T = sb("x1T", [P, CC, T])
        route = sb("route", [P, TT, NE])
        pick = sb("pick", [P, TT, NE])
        pick_min = sb("pick_min", [P, TT])
        onehot = sb("onehot", [P, TT, NE], BF16)
        next_row = sb("next_row", [P, NE])
        region0 = sb("region0", [P, NE])
        place = sb("place", [P, TT, NE])
        dest = sb("dest", [P, TT])
        dest_i = sb("dest_i", [P, TT], I32)
        token_no = sb("token_no", [P, TT])
        t8 = sb("t8", [P, 4, NE])
        t8i = sb("t8i", [P, NE], I32)
        one8 = sb("one8", [P, NE])
        sel = sb("sel", [P, 2, NT, NE])
        tab = sb("tab", [P, 4, NT])
        row_tab = sb("row_tab", [P, NT], I32)
        expert_tab = sb("expert_tab", [P, NT], I32)
        pad_tab = sb("pad_tab", [P, NE], I32)
        xs = sb("xs", [P, 2, ROW])
        kept = sb("kept", [P, 2, ROW])
        xsT = sb("xsT", [P, 2, CC * P])
        silu = sb("silu", [P, 2, NI])
        hh = sb("hh", [P, 2, NI])
        hT = sb("hT", [P, 2, NI])
        z = sb("z", [P, 2, C])
        zstats = sb("zstats", [P, 2, 6])
        zmv = sb("zmv", [P, 2, 2])
        zrstd = sb("zrstd", [P, 2])
        zi = sb("zi", [P, 2], I32)

        pa = ctx.enter_context(nc.psum_tensor("pa", [P, 2, 2, T], F32))
        pb = ctx.enter_context(nc.psum_tensor("pb", [P, 2, T], F32))
        pv = ctx.enter_context(nc.psum_tensor("pv", [P, 2, T], F32))

        y2 = [pb[:, 1, 0:C], pv[:, 1, 0:C]]

        const_done = sem("const_done")
        ones_done = sem("ones_done")
        vv_ones = sem("vv_ones")
        stack_ones = sem("stack_ones")
        wq_in, wc_in, wk_in = sem("wq_in"), sem("wc_in"), sem("wk_in")
        weights_in = sem("weights_in")
        gate_up_in = sem("gate_up_in")
        down_in = sem("down_in")
        xt_in = sem("xt_in")
        xr_in = sem("xr_in")
        unit_ready = sem("unit_ready")
        unit_read = [sem("unit0_read"), sem("unit1_read")]
        high_ready = sem("high_ready")
        mid_ready = sem("mid_ready")
        low_ready = sem("low_ready")
        parts_out = sem("parts_out")
        stack_in = [sem(f"stack_in{g}") for g in range(NG)]
        max_parts_ready = sem("max_parts_ready")
        max_out = sem("max_out")
        max_in = [sem("max_in0"), sem("max_in1")]
        scores_ready = sem("scores_ready")
        exp_done = sem("exp_done")
        masked = sem("masked")
        pv_done = sem("pv_done")
        oT_ready = sem("oT_ready")
        xr_biased = sem("xr_biased")
        var_ready = sem("var_ready")
        rstd_ready = sem("rstd_ready")
        x1_ready = sem("x1_ready")
        onehot_ready = sem("onehot_ready")
        dest_ready = sem("dest_ready")
        scattered = sem("scattered")
        tables_ready = sem("tables_ready")
        pads_out = sem("pads_out")
        dve_chain = sem("dve_chain")
        pool_chain = sem("pool_chain")
        xs_in = [sem("xs_in0"), sem("xs_in1")]
        rows_kept = sem("rows_kept")
        xsT_psum = sem("xsT_psum")
        xsT_ready = sem("xsT_ready")
        gate_ready = sem("gate_ready")
        up_ready = sem("up_ready")
        silu_done = sem("silu_done")
        h_ready = sem("h_ready")
        hT_psum = sem("hT_psum")
        hT_ready = sem("hT_ready")
        y2_ready = sem("y2_ready")
        z_ready = sem("z_ready")
        zvar_ready = sem("zvar_ready")
        zrstd_ready = sem("zrstd_ready")
        zstats_ready = sem("zstats_ready")
        zeps_ready = sem("zeps_ready")
        z_normed = sem("z_normed")
        out_done = [sem("out_done0"), sem("out_done1")]

        def slot(idx):
            return idx % 2

        def wait_read(engine, n, b, per):
            earlier_ones = n // 2 - (U0 if n % 2 == 0 else 0)
            engine.wait_ge(unit_read[n % 2], earlier_ones + 1 + b * (per // 2))

        def wait_banks(pe, n, b, per):
            earlier_ones = n // 2 - (U0 if n % 2 == 0 else 0)
            wait(pe, unit_read[n % 2], earlier_ones + b * (per // 2))

        def apart(engine):
            engine.nop(nofuse=True)

        block = ctx.enter_context(nc.Block())

        @block.sync
        def _(sp):
            sp.dma_start(xt[:], tokens[:, 0:TT, :]).then_inc(xt_in, 16)
            sp.dma_start(wc[:], Wc.rearrange("(k p) n -> p k n", p=P)).then_inc(wc_in, 16)
            sp.dma_start(wv[:], Wv).then_inc(weights_in, 16)
            sp.dma_start(wo[:], Wo.rearrange("(k p) n -> p k n", p=P)).then_inc(weights_in, 16)
            sp.dma_start(wr[:], router_w.rearrange("(k p) n -> p k n", p=P)).then_inc(weights_in, 16)
            sp.dma_start(bias[:], bo.rearrange("(o n) -> o n", o=1).to_broadcast([P, C])).then_inc(weights_in, 16)

            def spill_parts(bn):
                for i in range(2):
                    for s, made in ((0, high_ready), (1, mid_ready), (2, low_ready)):
                        sp.wait_ge(made, bn * 2 + i + 1)
                        dst = qk_dram[bass.ds(bn, 1), i, s].rearrange("o (k p) t -> p (o k) t", p=P)
                        sp.dma_start(dst, parts[i][s][:]).then_inc(parts_out, 16)

            def load_stacks(bn, g):
                for i, stack in enumerate((q_stack, k_stack)):
                    row = 0
                    for r, terms in enumerate(RUNS):
                        s0, s1 = (r, r + 1) if i == 0 else (0, terms)
                        src = qk_dram[bass.ds(bn, 1), i, s0:s1, g * GH * HS:(g + 1) * GH * HS, :]
                        src = src.rearrange("o s (d h) t -> (o s) d (h t)", d=HS)
                        if i == 0:
                            src = src.to_broadcast([terms, HS, GH * T])
                        sp.dma_start(stack[row:row + terms * HS, g * GH:(g + 1) * GH, :].rearrange("k h t -> k (h t)"), src)\
                            .then_inc(stack_in[g], 16)
                        row += terms * HS

            def move_maxima(b, g, unit, per):
                G = b * NG + g
                wait_read(sp, unit, b, per)
                sp.dma_start(max_dram[bass.ds(G, 1)].rearrange("o r p -> (o r) p"), maxT[:]).then_inc(max_out, 16)
                sp.wait_ge(max_out, G * 16 + 16)
                g4 = g % NG
                src = max_dram[bass.ds(G, 1)].rearrange("o (s r) p -> (o s) (r p)", s=3)
                dst = q_stack[KS:KM, g4 * GH:(g4 + 1) * GH, :].rearrange("s h t -> s (h t)")
                sp.dma_start(dst, src).then_inc(max_in[g % 2], 16)

            def load_expert(e, dst, w):
                sp.dma_start(dst[:, bass.ds(e, 1)].rearrange("p o k n -> p (o k) n"),
                             w[bass.ds(e, 1)].rearrange("o (k p) n -> p (o k) n", p=P)).then_inc(gate_up_in, 16)

            def load_residual(b):
                wait(sp, scattered, b * 64)
                sp.dma_start(xr[:, :, 0:C], tokens[:, bass.ds(b * TT, TT), :]).then_inc(xr_in, 16)

            spill_parts(0)
            sp.wait_ge(parts_out, 96)
            for g in range(NG - 1):
                load_stacks(0, g)
            move_maxima(0, 0, unit_numbers(PROLOGUE, "M", U0)[0], 0)
            load_stacks(0, NG - 1)

            def run(b, order, const, per):
                first, last = (isinstance(b, int) and b == k for k in (0, NB - 1))
                if not last:
                    sp.wait_ge(high_ready, b * 2 + 1)
                    sp.dma_start(xt[:], tokens[:, bass.ds((b + 1) * TT, TT), :]).then_inc(xt_in, 16)
                for g in range(NG):
                    if not (last and g == NG - 1):
                        move_maxima(b, g + 1, unit_numbers(order, "M", const)[g], per)
                    if g == 0 and not first:
                        sp.wait_ge(scores_ready, b * NG * BANKS)
                        apart(sp)
                        load_stacks(b, NG - 1)
                        load_residual(b - 1)
                    if g > 0 and not last:
                        if g == 1:
                            sp.wait_ge(parts_out, (b + 1) * 96 + 96)
                            apart(sp)
                        sp.wait_ge(scores_ready, b * NG * BANKS + g * BANKS)
                        apart(sp)
                        load_stacks(b + 1, g - 1)
                    if g == 0 and not last:
                        spill_parts(b + 1)
                    dst, w = ((gate, gate_w), (up, up_w))[g % 2]
                    load_expert(b * 2 + g // 2, dst, w)

            bodies(run, sp.Fori)
            load_residual(NB - 1)
            sp.wait_ge(scores_ready, NB * NG * BANKS)
            sp.dma_start(down[:], down_w.rearrange("e (k p) n -> p e k n", p=P)).then_inc(down_in, 16)

            sp.wait_ge(tables_ready, 1)
            for e in range(NE):
                row = sp.value_load(pad_tab[0:1, e:e + 1], min_val=e * REGION, max_val=(e + 1) * REGION - P)
                sp.dma_start(rows_dram[bass.ds(row, P), :], padding[:]).then_inc(pads_out, 16)
            sp.dma_start(rows_dram[PAD_ROW:PAD_ROW + P, :], padding[:]).then_inc(pads_out, 16)
            sp.wait_ge(pads_out, (NE + 1) * 16)
            sp.wait_ge(scattered, NB * 64)

            def load_tile(pair, odd):
                i = 2 * pair + odd
                row = sp.value_load(row_tab[0:1, bass.ds(i, 1)], min_val=0, max_val=PAD_ROW)
                wait(sp, xsT_psum, i - 1)
                wait(sp, rows_kept, i - 1)
                sp.dma_start(xs[:, odd, :], rows_dram[bass.ds(row, P), :]).then_inc(xs_in[odd], 16)

            load_tile(0, 0)
            load_tile(0, 1)
            with sp.Fori(1, PAIRS) as p:
                load_tile(p, 0)
                load_tile(p, 1)
            load_tile(PAIRS, 0)
            sp.wait_ge(out_done[0], (NT + 1) // 2 * 16)
            sp.wait_ge(out_done[1], NT // 2 * 16)

        @block.tensor
        def _(pe):
            pe.wait_ge(const_done, 1)

            def run(b, order, const, per):
                n, unit = const, {}
                first = order is first_body
                for name, g, u in order:
                    G = b * NG + g
                    s = slot(n)
                    if name in UNITS:
                        wait_banks(pe, n, b, per)
                        unit[name] = n
                        n += 1
                    if order is PROLOGUE and name in ("Q", "C", "K"):
                        pe.wait_ge({"Q": wq_in, "C": wc_in, "K": wk_in}[name], 16)
                    if order is PROLOGUE and name == "V":
                        pe.wait_ge(weights_in, 4 * 16)
                    if name == "X":
                        pe.wait_ge(xt_in, projected(b, g) * 16 + 16)
                        for t in range(TT):
                            for c in range(CC):
                                last = nc.tensor.transpose(pa[:, s, c, t * P:(t + 1) * P],
                                                           xt[:, t, c * P:(c + 1) * P], ident[:])
                    elif name == "Q":
                        wait_read(pe, unit["X"], b, per)
                        for m in range(CC):
                            for c in range(CC):
                                last = nc.tensor.matmul(pa[:, s, m, :], wq[:, c, m * P:(m + 1) * P], xT[:, c, :],
                                                        start=(c == 0), stop=(c == CC - 1))
                    elif name == "C":
                        for c in range(CC):
                            last = nc.tensor.matmul(pa[:, s, 0, :], wc[:, c, :], xT[:, c, :],
                                                    start=(c == 0), stop=(c == CC - 1))
                    elif name == "K":
                        wait_read(pe, unit["C"], b, per)
                        for m in range(CC):
                            last = nc.tensor.matmul(pa[:, s, m, :], wk[:, m * P:(m + 1) * P], cT[:],
                                                    start=True, stop=True)
                    elif name == "V":
                        for t in range(TT):
                            last = nc.tensor.matmul(pa[:, s, t // 2, t % 2 * C:(t % 2 + 1) * C],
                                                    cT[:, t * P:(t + 1) * P], wv[:], start=True, stop=True)
                    elif name == "S":
                        g4 = (g + 2) % NG
                        if u == 0:
                            bs = b if g + 2 < NG else b + 1
                            pe.wait_ge(stack_in[g4], (bs + 1) * 2 * len(RUNS) * 16)

                        def scores(dst, h, qt):
                            hh_ = g4 * GH + h
                            w = (qt + 1) * P
                            nc.tensor.matmul(dst[:, 0:w], q_stack[0:KS, hh_, qt * P:w], k_stack[0:KS, hh_, 0:w],
                                             start=True, stop=False)
                            return nc.tensor.matmul(dst[:, qt * P:w], ident_b[:], causal[:], start=False, stop=True)

                        if u == 0:
                            for h in range(GH):
                                last = scores(pa[:, s, h // 2, h % 2 * 2 * P:(h % 2 + 1) * 2 * P], h, 1)
                        elif u < 3:
                            for j in range(2):
                                scores(pa[:, s, j, 0:3 * P], 2 * (u - 1) + j, 2)
                                last = scores(pa[:, s, j, 3 * P:T], 2 * (u - 1) + j, 0)
                        else:
                            for j in range(2):
                                last = scores(pa[:, s, j, :], 2 * (u - 3) + j, 3)
                    elif name == "M":
                        pe.wait_ge(max_parts_ready, G + 2)
                        apart(pe)
                        last = nc.tensor.transpose(pa[0:3 * GH * TT, s, 0, 0:P // 2].bitcast(BF16),
                                                   max_parts[:, :, :, :].rearrange("p s h t -> p (s h t)"), ident_b[:])
                    elif name == "B":
                        if u == 0 and first and g == 0:
                            pe.wait_ge(stack_ones, 1)
                        if u == 0:
                            pe.wait_ge(max_in[g % 2], b * 32 + g // 2 * 16 + 16)
                        wait(pe, exp_done, G * BANKS + u - 1)

                        def turned(h, kt, col):
                            hh_ = g * GH + h
                            w = T - kt * P
                            return nc.tensor.matmul(pb[:, u % 2, col:col + w], k_stack[0:KM, hh_, kt * P:(kt + 1) * P],
                                                    q_stack[0:KM, hh_, kt * P:T], start=True, stop=True)

                        if u < 4:
                            last = turned(u, 0, 0)
                        elif u < 8:
                            turned(u - 4, 1, 0)
                            last = turned(u - 4, 3, 3 * P)
                        else:
                            for j in range(2):
                                last = turned(2 * (u - 8) + j, 2, j * 2 * P)
                        last.then_inc(scores_ready, 1)
                    elif name == "PV":
                        if u == 2:
                            G = G - 1
                        bank = (g - (u == 2)) % 2
                        g4 = (g - (u == 2)) % NG
                        if u == 0:
                            wait(pe, oT_ready, G - 1)
                        if u == 0 and g == 0 and "V" in unit:
                            wait_read(pe, unit["V"], b, per)
                        pe.wait_ge(masked, G * 3 + u + 1)
                        for kt in ((0,), (1, 3), (2,))[u]:
                            for h in range(GH):
                                hh_ = g4 * GH + h
                                if kt == 0:
                                    moving = probs[:, h, :]
                                elif kt == 2:
                                    moving = probs[:, 8 + h // 2, h % 2 * 2 * P:(h % 2 + 1) * 2 * P]
                                else:
                                    moving = probs[:, 4 + h, 0:3 * P] if kt == 1 else probs[:, 4 + h, 3 * P:T]
                                last = nc.tensor.matmul(pv[32 * h:32 * h + 32, bank, kt * P:T],
                                                        vv[:, kt, hh_ * VW:hh_ * VW + 32], moving,
                                                        start=(kt == 0), stop=(kt == 2))
                        last.then_inc(pv_done, 1)
                    elif name == "OT":
                        pe.wait_ge(oT_ready, G)
                        for t in range(TT):
                            last = nc.tensor.transpose(pa[:, s, 0, t * P:(t + 1) * P],
                                                       oT[:, (g - 1) % 2, t * P:(t + 1) * P], ident[:])
                    elif name == "YT":
                        wait_read(pe, unit["OT"], b, per)
                        for t in range(TT):
                            for c in range(CC):
                                last = nc.tensor.transpose(pa[:, s, c, t * P:(t + 1) * P],
                                                           y[:, t, c * P:(c + 1) * P], ident[:])
                    elif name == "WO":
                        wait_read(pe, unit["YT"], b, per)
                        for t in range(TT):
                            for c in range(CC):
                                last = nc.tensor.matmul(pa[:, s, t // 2, t % 2 * C:(t % 2 + 1) * C],
                                                        yT[:, c, t * P:(t + 1) * P], wo[:, c, :],
                                                        start=(c == 0), stop=(c == CC - 1))
                    elif name == "X1T":
                        pe.wait_ge(x1_ready, past(b, g))
                        for t in range(TT):
                            for c in range(CC):
                                last = nc.tensor.transpose(pa[:, s, c, t * P:(t + 1) * P],
                                                           xr[:, t, c * P:(c + 1) * P], ident[:])
                    elif name == "R":
                        wait_read(pe, unit["X1T"], b, per)
                        for t in range(TT):
                            for c in range(CC):
                                last = nc.tensor.matmul(pa[:, s, 0, t * NE:(t + 1) * NE],
                                                        x1T[:, c, t * P:(t + 1) * P], wr[:, c, :],
                                                        start=(c == 0), stop=(c == CC - 1))
                    elif name == "RK":
                        pe.wait_ge(onehot_ready, past(b, g))
                        for t in range(TT + 1):
                            dst = pa[:, s, 0, t * NE:(t + 1) * NE]
                            for t2 in range(min(t, TT)):
                                last = nc.tensor.matmul(dst, ones_b[:], onehot[:, t2, :], start=(t2 == 0),
                                                        stop=(t == TT and t2 == TT - 1))
                            if t < TT:
                                last = nc.tensor.matmul(dst, earlier[:], onehot[:, t, :], start=(t == 0), stop=True)
                    if name in UNITS:
                        last.then_inc(unit_ready, 1)

            run(0, PROLOGUE, U0, 0)
            bodies(run, pe.Fori)
            run(NB - 1, EPILOGUE, U_END, 0)

            pe.wait_ge(gate_up_in, 2 * NE * 16)
            pe.wait_ge(tables_ready, 1)

            def expert_of(i):
                return pe.value_load(expert_tab[0:1, bass.ds(i, 1)], min_val=0, max_val=NE - 1)

            def turn_rows(pair, odd):
                i = 2 * pair + odd
                pe.wait_ge(xs_in[odd], pair * 16 + 16)
                wait(pe, xsT_ready, i)
                for c in range(CC):
                    last = nc.tensor.transpose(pv[:, 0, c * P:(c + 1) * P], xs[:, odd, c * P:(c + 1) * P], ident[:])
                last.then_inc(xsT_psum, 1)

            def times(dst, rows, weights, expert, chunks):
                for c in range(chunks):
                    last = nc.tensor.matmul(dst, rows[:, c * P:(c + 1) * P],
                                            weights[:, bass.ds(expert, 1), c, :].rearrange("p o n -> p (o n)"),
                                            start=(c == 0), stop=(c == chunks - 1))
                return last

            def gate_of(pair, odd, expert):
                i = 2 * pair + odd
                pe.wait_ge(xsT_ready, i + 1)
                wait(pe, silu_done, i - 1)
                times(pa[:, odd, 0, :], xsT[:, odd, :], gate, expert, CC).then_inc(gate_ready, 1)

            def up_of(pair, odd, expert):
                i = 2 * pair + odd
                wait(pe, h_ready, i - 1)
                times(pa[:, odd, 1, :], xsT[:, odd, :], up, expert, CC).then_inc(up_ready, 1)

            def turn_inner(pair, odd):
                i = 2 * pair + odd
                pe.wait_ge(h_ready, i + 1)
                wait(pe, hT_ready, i)
                for c in range(IC):
                    last = nc.tensor.transpose(pb[:, 0, c * P:(c + 1) * P], hh[:, odd, c * P:(c + 1) * P], ident[:])
                last.then_inc(hT_psum, 1)

            def down_of(pair, odd):
                i = 2 * pair + odd
                expert = expert_of(i)
                pe.wait_ge(hT_ready, i + 1)
                wait(pe, z_ready, i - 1)
                times(y2[odd], hT[:, odd, :], down, expert, IC).then_inc(y2_ready, 1)

            def step(pair, odd, last=False):
                before = (pair, 0) if odd else (pair - 1, 1)
                expert = expert_of(2 * pair + odd)
                gate_of(pair, odd, expert)
                turn_inner(*before)
                up_of(pair, odd, expert)
                if not last:
                    turn_rows(*((pair + 1, 0) if odd else (pair, 1)))
                down_of(*before)

            turn_rows(0, 0)
            expert = expert_of(0)
            gate_of(0, 0, expert)
            up_of(0, 0, expert)
            turn_rows(0, 1)
            pe.wait_ge(down_in, 16)
            step(0, 1)
            with pe.Fori(1, PAIRS) as p:
                step(p, 0)
                step(p, 1)
            step(PAIRS, 0, last=True)
            turn_inner(PAIRS, 0)
            down_of(PAIRS, 0)

        @block.scalar
        def _(act):
            act.dma_start(wq[:], Wq.rearrange("(k p) n -> p k n", p=P)).then_inc(wq_in, 16)
            act.dma_start(wk[:], Wk).then_inc(wk_in, 16)
            nc.scalar.preload_act_table(ACT.Exp)
            act.wait_ge(vv_ones, 1)

            def run(b, order, const, per):
                n = const
                for name, g, u in order:
                    G = b * NG + g
                    s = slot(n)
                    n += name in UNITS
                    ready = n - U0 + b * per
                    if name == "X":
                        act.wait_ge(unit_ready, ready)
                        nc.scalar.activation(xT[:], pa[:, s, :, :], ACT.Copy)\
                            .then_inc(unit_read[s], 1)
                    elif name in ("Q", "K"):
                        i = int(name == "K")
                        act.wait_ge(unit_ready, ready)
                        wait(act, parts_out, projected(b, g) * 96)
                        nc.scalar.activation(parts[i][0][:], pa[:, s, :, :], ACT.Copy).then_inc(high_ready, 1)
                    elif name == "C":
                        act.wait_ge(unit_ready, ready)
                        nc.scalar.activation(cT[:], pa[:, s, 0, :], ACT.Copy)\
                            .then_inc(unit_read[s], 1)
                    elif name == "V":
                        act.wait_ge(unit_ready, ready)
                        v4 = vv[:, :, 0:NH * VW].rearrange("p t (h d) -> p t h d", d=VW)
                        for t in range(TT):
                            last = nc.scalar.activation(v4[:, t, :, 0:HS],
                                                        pa[:, s, t // 2, t % 2 * C:(t % 2 + 1) * C]
                                                        .rearrange("p (h d) -> p h d", d=HS), ACT.Copy)
                        last.then_inc(unit_read[s], 1)
                    elif name == "B":
                        act.wait_ge(scores_ready, G * BANKS + u + 1)
                        wait(act, pv_done, (G - 1) * 3 + (1 if u < 4 else 2 if u < 8 else 3))
                        nc.scalar.activation(probs[:, u, :], pb[:, u % 2, :], ACT.Exp, scale=SCORE_SCALE)\
                            .then_inc(exp_done, 1)
                    elif name == "PV" and u == 2:
                        act.wait_ge(pv_done, G * 3)
                        nc.scalar.activation(oT[:, (g - 1) % 2, :], pv[:, (g - 1) % 2, :], ACT.Copy)\
                            .then_inc(oT_ready, 1)
                    elif name == "M":
                        act.wait_ge(unit_ready, ready)
                        wait(act, max_out, (G + 1) * 16)
                        nc.scalar.activation(maxT[:], pa[0:3 * GH * TT, s, 0, 0:P // 2].bitcast(BF16), ACT.Copy)\
                            .then_inc(unit_read[s], 1)
                    elif name == "YT":
                        act.wait_ge(unit_ready, ready)
                        nc.scalar.activation(yT[:], pa[:, s, :, :], ACT.Copy)\
                            .then_inc(unit_read[s], 1)
                    elif name == "X1T":
                        act.wait_ge(unit_ready, ready)
                        nc.scalar.activation(x1T[:], pa[:, s, :, :], ACT.Copy)\
                            .then_inc(unit_read[s], 1)
                    elif name == "R":
                        act.wait_ge(unit_ready, ready)
                        nc.scalar.activation(route[:, :, :].rearrange("p t e -> p (t e)"), pa[:, s, 0, 0:TT * NE],
                                             ACT.Exp, scale=-1.0)\
                            .then_inc(unit_read[s], 1)

            run(0, PROLOGUE, U0, 0)
            bodies(run, act.Fori)
            run(NB - 1, EPILOGUE, U_END, 0)

            def rows_turned(pair, odd):
                i = 2 * pair + odd
                act.wait_ge(xsT_psum, i + 1)
                wait(act, up_ready, i - 1)
                nc.scalar.activation(xsT[:, odd, :], pv[:, 0, 0:CC * P], ACT.Copy).then_inc(xsT_ready, 1)

            def inner(pair, odd):
                i = 2 * pair + odd
                act.wait_ge(gate_ready, i + 1)
                wait(act, h_ready, i - 1)
                nc.scalar.activation(silu[:, odd, :], pa[:, odd, 0, :], ACT.Silu).then_inc(silu_done, 1)

            def inner_turned(pair, odd):
                i = 2 * pair + odd
                act.wait_ge(hT_psum, i + 1)
                wait(act, y2_ready, i - 1)
                nc.scalar.activation(hT[:, odd, :], pb[:, 0, :], ACT.Copy).then_inc(hT_ready, 1)

            def step(pair, odd, last=False):
                inner(pair, odd)
                inner_turned(*((pair, 0) if odd else (pair - 1, 1)))
                if not last:
                    rows_turned(*((pair + 1, 0) if odd else (pair, 1)))

            nc.scalar.preload_act_table(ACT.Silu)
            rows_turned(0, 0)
            inner(0, 0)
            rows_turned(0, 1)
            step(0, 1)
            with act.Fori(1, PAIRS) as p:
                step(p, 0)
                step(p, 1)
            step(PAIRS, 0, last=True)
            inner_turned(PAIRS, 0)

        @block.vector
        def _(dve):
            chain = Chain(dve, dve_chain, DVE_LINKS)
            V = nc.vector

            def run(b, order, const, per):
                n = const
                for name, g, u in order:
                    G = b * NG + g
                    s = slot(n)
                    n += name in UNITS
                    ready = n - U0 + b * per
                    if name in ("Q", "K"):
                        i = int(name == "K")
                        two = projected(b, g) * 2 + i
                        dve.wait_ge(high_ready, two + 1)
                        wait(dve, low_ready, two)
                        V.tensor_tensor(rest[:], pa[:, s, :, :], parts[i][0][:], ALU.subtract).then_inc(unit_read[s], 1)
                        wait_read(dve, n - 1, b, per)
                        V.tensor_copy(parts[i][1][:], rest[:]).then_inc(mid_ready, 1)
                    elif name == "S":
                        dve.wait_ge(unit_ready, ready)
                        if u == 0:
                            V.tensor_reduce(row_max[:, :, 1], pa[:, s, :, :].rearrange("p k (h t) -> p (k h) t", h=2),
                                            AX.X, ALU.max).then_inc(unit_read[s], 1)
                        elif u < 3:
                            h = 2 * (u - 1)
                            V.tensor_reduce(row_max[:, h:h + 2, 2], pa[:, s, :, 0:3 * P], AX.X, ALU.max)
                            V.tensor_reduce(row_max[:, h:h + 2, 0], pa[:, s, :, 3 * P:T], AX.X, ALU.max)\
                                .then_inc(unit_read[s], 1)
                        else:
                            h = 2 * (u - 3)
                            last = V.tensor_reduce(row_max[:, h:h + 2, 3], pa[:, s, :, :], AX.X, ALU.max)
                            last.then_inc(unit_read[s], 1)
                        if u == 4:
                            wait_read(dve, n - 1, b, per)
                            high, mid, low = (max_parts[:, i, :, :] for i in range(3))
                            chain.link(V.tensor_scalar(high, row_max[:], -1.0, None, ALU.mult))
                            chain.link(V.scalar_tensor_tensor(max_rest[:], row_max[:], -1.0, high, ALU.mult, ALU.subtract))
                            chain.link(V.tensor_copy(mid, max_rest[:]))
                            V.tensor_tensor(low, max_rest[:], mid, ALU.subtract).then_inc(max_parts_ready, 1)
                    elif name == "OT":
                        dve.wait_ge(unit_ready, ready)
                        o4 = pa[:, s, 0, :].rearrange("p (t h d) -> p t h d", t=TT, h=GH)
                        chain.link(V.reciprocal(rsum[:], o4[:, :, :, HS]))
                        ch = (g - 1) % NG * GH * HS
                        y4 = y[:, :, ch:ch + GH * HS].rearrange("p t (h d) -> p t h d", h=GH)
                        V.tensor_tensor(y4, o4[:, :, :, 0:HS],
                                        rsum[:, :, :].rearrange("p t (h o) -> p t h o", o=1).to_broadcast([P, TT, GH, HS]),
                                        ALU.mult).then_inc(unit_read[s], 1)
                    elif name == "WO":
                        dve.wait_ge(unit_ready, ready)
                        dve.wait_ge(xr_biased, past(b, g))
                        last = V.tensor_tensor(xr[:, :, 0:C], pa[:, s, :, :].rearrange("p k (t c) -> p (k t) c", t=2),
                                               xr[:, :, 0:C], ALU.add)
                        last.then_inc(unit_read[s], 1)
                        wait_read(dve, n - 1, b, per)
                        for t in range(TT):
                            last = V.bn_stats(stats[:, t, :], xr[:, t, 0:C])
                        chain.link(last)
                        apart(dve)
                        for t in range(TT):
                            last = V.bn_aggr(mean_var[:, t, :], stats[:, t, :])
                        last.then_inc(var_ready, 1)
                    elif name == "LN":
                        dve.wait_ge(rstd_ready, past(b, g))
                        for t in range(TT):
                            last = V.tensor_scalar(xr[:, t, 0:C], xr[:, t, 0:C], mean_var[:, t, 0:1], rstd[:, t:t + 1],
                                                   ALU.subtract, ALU.mult)
                        last.then_inc(x1_ready, 1)
                    elif name == "R":
                        wait_read(dve, n - 1, b, per)
                        chain.link(V.tensor_scalar(route[:], route[:], 1.0, None, ALU.add))
                        chain.link(V.reciprocal(route[:], route[:]))
                        chain.link(V.tensor_reduce(xr[:, :, C], route[:], AX.X, ALU.max))
                        chain.link(V.tensor_tensor(pick[:], route[:],
                                                   xr[:, :, C:C + 1].to_broadcast([P, TT, NE]), ALU.is_equal))
                        e8 = expert8[:, :].rearrange("p (o e) -> p o e", o=1).to_broadcast([P, TT, NE])
                        chain.link(V.tensor_tensor(pick[:], pick[:], e8, ALU.mult))
                        chain.link(V.tensor_reduce(pick_min[:], pick[:], AX.X, ALU.min))
                        V.tensor_tensor(onehot[:], e8, pick_min[:, :].rearrange("p (t o) -> p t o", o=1)
                                        .to_broadcast([P, TT, NE]), ALU.is_equal).then_inc(onehot_ready, 1)
                    elif name == "RK":
                        dve.wait_ge(unit_ready, ready)
                        ranks = pa[:, s, 0, 0:(TT + 1) * NE].rearrange("p (t e) -> p t e", e=NE)
                        nr = next_row[:, :].rearrange("p (o e) -> p o e", o=1)
                        chain.link(V.tensor_tensor(place[:], ranks[:, 0:TT, :], nr.to_broadcast([P, TT, NE]), ALU.add))
                        chain.link(V.tensor_tensor(place[:], place[:], onehot[:], ALU.mult))
                        V.tensor_tensor(nr, ranks[:, TT:TT + 1, :], nr, ALU.add).then_inc(unit_read[s], 1)
                        chain.link(V.tensor_reduce(dest[:], place[:], AX.X, ALU.add))
                        chain.link(V.tensor_copy(xr[:, :, C + 1], token_no[:]))
                        chain.link(V.tensor_scalar(token_no[:], token_no[:], float(T), None, ALU.add))
                        V.tensor_copy(dest_i[:], dest[:]).then_inc(dest_ready, 1)

            V.memset(vv[:], 1.0).then_inc(vv_ones, 1)
            V.memset(padding[:, 0:C + 1], 0.0)
            V.memset(padding[:, C + 1:ROW], NO_TOKEN)
            V.memset(minus_half[:], -0.5)
            V.memset(one8[:], 1.0).then_inc(ones_done, 1)
            dve.wait_ge(ones_done, 1)
            dve.wait_ge(const_done, 1)
            chain.link(V.tensor_scalar(region0[:], expert8[:], float(NE), float(REGION), ALU.add, ALU.mult))
            chain.link(V.tensor_copy(next_row[:], region0[:]))

            run(0, PROLOGUE, U0, 0)
            bodies(chain.counted(run), dve.Fori)
            run(NB - 1, EPILOGUE, U_END, 0)

            rows, tiles, upto, before = (t8[:, k, :] for k in range(4))
            chain.link(V.tensor_copy(pad_tab[:], next_row[:]))
            chain.link(V.tensor_tensor(rows, next_row[:], region0[:], ALU.subtract))
            chain.link(V.tensor_scalar(rows, rows, float(P - 1), None, ALU.add))
            chain.link(V.tensor_copy(t8i[:], rows))
            chain.link(V.tensor_single_scalar(t8i[:], t8i[:], 7, ALU.arith_shift_right))
            chain.link(V.tensor_copy(tiles, t8i[:]))
            chain.link(V.tensor_tensor_scan(upto, one8[:], tiles, 0.0, ALU.mult, ALU.add))
            chain.link(V.tensor_tensor(before, upto, tiles, ALU.subtract))

            def by_tile(a):
                return a.rearrange("p (o e) -> p o e", o=1).to_broadcast([P, NT, NE])

            no = tile_no[:, :].rearrange("p (t o) -> p t o", o=1).to_broadcast([P, NT, NE])
            s0, s1 = sel[:, 0], sel[:, 1]
            chain.link(V.tensor_tensor(s0, no, by_tile(before), ALU.is_ge))
            chain.link(V.tensor_tensor(s1, no, by_tile(upto), ALU.is_lt))
            chain.link(V.tensor_tensor(s0, s0, s1, ALU.mult))
            chain.link(V.scalar_tensor_tensor(before, before, -float(P), region0[:], ALU.mult, ALU.add))
            chain.link(V.tensor_tensor(s1, s0, by_tile(before), ALU.mult))
            base, used, away, number = (tab[:, k, :] for k in range(4))
            chain.link(V.tensor_reduce(base, s1, AX.X, ALU.add))
            chain.link(V.tensor_reduce(used, s0, AX.X, ALU.add))
            chain.link(V.tensor_scalar(away, tile_no[:], float(P), -float(PAD_ROW), ALU.mult, ALU.add))
            chain.link(V.tensor_tensor(away, away, used, ALU.mult))
            chain.link(V.tensor_tensor(base, base, away, ALU.add))
            chain.link(V.tensor_scalar(base, base, float(PAD_ROW), None, ALU.add))
            chain.link(V.tensor_copy(row_tab[:], base))
            chain.link(V.tensor_tensor(s1, s0, by_tile(expert8[:, :]), ALU.mult))
            chain.link(V.tensor_reduce(number, s1, AX.X, ALU.add))
            chain.link(V.tensor_scalar(number, number, float(NE), float(NE - 1), ALU.add, ALU.min))
            V.tensor_copy(expert_tab[:], number).then_inc(tables_ready, 1)

            def inner(pair, odd):
                i = 2 * pair + odd
                dve.wait_ge(silu_done, i + 1)
                dve.wait_ge(up_ready, i + 1)
                wait(dve, hT_psum, i - 1)
                V.tensor_tensor(hh[:, odd, :], pa[:, odd, 1, :], silu[:, odd, :], ALU.mult).then_inc(h_ready, 1)

            def keep(pair, odd):
                dve.wait_ge(xs_in[odd], pair * 16 + 16)
                apart(dve)
                V.tensor_copy(kept[:, odd, :], xs[:, odd, :]).then_inc(rows_kept, 1)

            def outer(pair, odd):
                i = 2 * pair + odd
                dve.wait_ge(y2_ready, i + 1)
                dve.wait_ge(rows_kept, i + 1)
                wait(dve, out_done[odd], pair * 16)
                V.scalar_tensor_tensor(z[:, odd, :], y2[odd], kept[:, odd, C:C + 1], kept[:, odd, 0:C],
                                       ALU.mult, ALU.add).then_inc(z_ready, 1)
                V.tensor_copy(zi[:, odd:odd + 1], kept[:, odd, C + 1:C + 2])
                dve.wait_ge(z_ready, i + 1)
                V.bn_stats(zstats[:, odd, :], z[:, odd, :]).then_inc(zstats_ready, 1)
                dve.wait_ge(zstats_ready, i + 1)
                apart(dve)
                V.bn_aggr(zmv[:, odd, :], zstats[:, odd, :]).then_inc(zvar_ready, 1)

            def norm(pair, odd):
                i = 2 * pair + odd
                dve.wait_ge(zrstd_ready, i + 1)
                V.tensor_scalar(z[:, odd, :], z[:, odd, :], zmv[:, odd, 0:1], zrstd[:, odd:odd + 1],
                                ALU.subtract, ALU.mult).then_inc(z_normed, 1)

            keep(0, 0)
            keep(0, 1)
            inner(0, 0)
            inner(0, 1)
            outer(0, 0)
            keep(1, 0)
            with dve.Fori(1, PAIRS) as p:
                inner(p, 0)
                norm(p - 1, 0)
                outer(p - 1, 1)
                keep(p, 1)
                inner(p, 1)
                norm(p - 1, 1)
                outer(p, 0)
                keep(p + 1, 0)
            inner(PAIRS, 0)
            norm(PAIRS - 1, 0)
            outer(PAIRS - 1, 1)
            norm(PAIRS - 1, 1)
            outer(PAIRS, 0)
            norm(PAIRS, 0)

        @block.gpsimd
        def _(pool):
            g_ = nc.gpsimd
            chain = Chain(pool, pool_chain, POOL_LINKS)
            g_.memset(ident[:], 0.0)
            g_.memset(ident_b[:], 0.0)
            g_.memset(causal[:], 0.0)
            g_.memset(earlier[:], 1.0)
            g_.memset(ones_b[:], 1.0)
            g_.iota(expert8[:], [[1, NE]], base=-NE, channel_multiplier=0, allow_small_or_imprecise_dtypes=True)
            g_.iota(tile_no[:], [[1, NT]], base=0, channel_multiplier=0, allow_small_or_imprecise_dtypes=True)
            chain.link(g_.iota(token_no[:], [[P, TT]], base=0, channel_multiplier=1,
                               allow_small_or_imprecise_dtypes=True))
            for m in (ident, ident_b):
                g_.affine_select(out=m[:], in_=m[:], pattern=[[-1, P]], compare_op=ALU.not_equal, fill=1.0,
                                 base=0, channel_multiplier=1)
            g_.affine_select(out=causal[:], in_=causal[:], pattern=[[-1, P]], compare_op=ALU.is_ge, fill=MASKED,
                             base=0, channel_multiplier=1)
            g_.affine_select(out=earlier[:], in_=earlier[:], pattern=[[1, P]], compare_op=ALU.is_gt, fill=0.0,
                             base=0, channel_multiplier=-1).then_inc(const_done, 1)

            pool.wait_ge(const_done, 1)
            g_.memset(k_stack[KS:KM, :, :], 1.0).then_inc(stack_ones, 1)

            def clear_later(view, blocks):
                return g_.affine_select(out=view, in_=view, pattern=[[0, k] for k in blocks] + [[1, P]],
                                        compare_op=ALU.is_ge, fill=0.0, base=0, channel_multiplier=-1)

            def run(b, order, const, per):
                for name, g, u in order:
                    G = b * NG + g
                    if name in ("QL", "KL"):
                        i = int(name == "KL")
                        pool.wait_ge(mid_ready, projected(b, g) * 2 + i + 1)
                        g_.tensor_tensor(parts[i][2][:], rest[:], parts[i][1][:], ALU.subtract).then_inc(low_ready, 1)
                    elif name == "B" and u in (3, 7, 9):
                        pool.wait_ge(exp_done, G * BANKS + u + 1)
                        apart(pool)
                        if u == 3:
                            last = clear_later(probs[:, 0:4, 0:P], [GH])
                        elif u == 7:
                            view = probs[:, 4:8, :].rearrange("p h (k q) -> p h k q", q=P)
                            clear_later(view[:, :, 0, :], [GH])
                            last = clear_later(view[:, :, 3, :], [GH])
                        else:
                            view = probs[:, 8:10, :].rearrange("p h (k q) -> p (h k) q", q=2 * P)
                            last = clear_later(view[:, :, 0:P], [GH])
                        last.then_inc(masked, 1)
                    elif name == "XB":
                        pool.wait_ge(xr_in, (past(b, g)) * 16)
                        g_.tensor_tensor(xr[:, :, 0:C], xr[:, :, 0:C],
                                         bias[:, :].rearrange("p (o c) -> p o c", o=1).to_broadcast([P, TT, C]),
                                         ALU.add).then_inc(xr_biased, 1)
                    elif name == "RV":
                        pool.wait_ge(var_ready, past(b, g))
                        apart(pool)
                        chain.link(g_.tensor_scalar(rstd[:], mean_var[:, :, 1], EPS, None, ALU.add))
                        g_.tensor_tensor(rstd[:], rstd[:], minus_half[:], ALU.pow).then_inc(rstd_ready, 1)
                    elif name == "SC":
                        if u == 0:
                            pool.wait_ge(dest_ready, past(b, g))
                            apart(pool)
                        g_.indirect_dma_start(out=rows_dram, out_offset=bass.IndirectOffsetOnAxis(dest_i[:, u:u + 1], 0),
                                              in_=xr[:, u, :], in_offset=None).then_inc(scattered, 16)

            pool.wait_ge(stack_ones, 1)
            pool.wait_ge(weights_in, 4 * 16)
            run(0, PROLOGUE, U0, 0)
            bodies(chain.counted(run), pool.Fori)
            run(NB - 1, EPILOGUE, U_END, 0)

            def finish(pair, odd):
                i = 2 * pair + odd
                pool.wait_ge(zvar_ready, i + 1)
                apart(pool)
                g_.tensor_scalar(zrstd[:, odd:odd + 1], zmv[:, odd, 1:2], EPS, None, ALU.add).then_inc(zeps_ready, 1)
                pool.wait_ge(zeps_ready, i + 1)
                g_.tensor_tensor(zrstd[:, odd:odd + 1], zrstd[:, odd:odd + 1], minus_half[:, 0:1], ALU.pow)\
                    .then_inc(zrstd_ready, 1)
                pool.wait_ge(z_normed, i + 1)
                apart(pool)
                g_.indirect_dma_start(out=out_rows, out_offset=bass.IndirectOffsetOnAxis(zi[:, odd:odd + 1], 0),
                                      in_=z[:, odd, :], in_offset=None, bounds_check=NTOK - 1, oob_is_err=False)\
                    .then_inc(out_done[odd], 16)

            finish(0, 0)
            finish(0, 1)
            with pool.Fori(1, PAIRS) as p:
                finish(p, 0)
                finish(p, 1)
            finish(PAIRS, 0)


_INS = ["L0_attn_x", "L0_attn_Wq", "L0_attn_Wc", "L0_attn_Wk", "L0_attn_Wv", "L0_attn_Wo", "L0_attn_bo",
        "L0_ffn_router_w", "L0_ffn_gate_w", "L0_ffn_up_w", "L0_ffn_down_w"]


def kernel(**inputs):
    import numpy as np
    import concourse.bacc as bacc
    from concourse.bass_utils import run_bass_kernel_spmd

    nc = bacc.Bacc("TRN2", target_bir_lowering=False, num_devices=1)
    arrays, args = {}, []
    for name in _INS:
        a = inputs[name]
        if name in ("L0_attn_Wq", "L0_attn_Wk"):
            a = np.asarray(a).reshape(-1, NG, GH, HS).transpose(0, 1, 3, 2).reshape(-1, C)
        a = np.ascontiguousarray(a)
        arrays[name + "_dram"] = a
        args.append(nc.dram_tensor(name + "_dram", a.shape, mybir.dt.from_np(a.dtype), kind="ExternalInput").ap())
    args.append(nc.dram_tensor("out_dram", (NB, T, C), F32, kind="ExternalOutput").ap())
    kernel_program(nc, *args)
    return run_bass_kernel_spmd(nc, [arrays], core_ids=[0]).results[0]["out_dram"]
```

```python
import concourse.bass as bass
from concourse import mybir
from contextlib import ExitStack

F32 = mybir.dt.float32
BF16 = mybir.dt.bfloat16
F32R = mybir.dt.float32r
I32 = mybir.dt.int32
ALU = mybir.AluOpType
ACT = mybir.ActivationFunctionType
AX = mybir.AxisListType

P = 128
NB, T, C = 4, 512, 256
NH, HS = 16, 16
NTOK = NB * T
TT = T // P
CC = C // P
GH = 4
NG = NH // GH
LAT = 128
NE, NI = 8, 512
IC = NI // P
RUNS = [3, 2, 1]
TERMS = sum(RUNS)
KS = TERMS * HS
KM = KS + 3
VW = HS + 1
SCORE_SCALE = HS ** -0.5
EPS = 1e-5
MASKED = -1e30
NT = NTOK // P + NE - 1
REGION = NTOK + P
PAD_ROW = NE * REGION
ROW = C + 2
NO_TOKEN = 4096.0
EARLY = -(-((NB - 1) * T - NE * (P - 1)) // P)
LATE = NT - EARLY
assert EARLY % 2 == 1 and LATE % 2 == 0
BANKS = 10


ORDER = [
    "LX B0 S0 B1 B2 PV2 B3 S1 M MM V0 LR V1 S2 S3 S4 LD XS B4 "
    "PV0 B5 B6 OT S5 S6 B7 S7 B8 Q0 QL0 Q1 QS0 QL1 C QS1 XB B9 S8 K0 LW KL0 K1 S9 KS0 PV1 KL1",
    "B0 KS1 S0 B1 B2 S1 YT0 PV2 M MM YT1 LD S2 B3 S3 B4 OT S4 B5 "
    "B6 PV0 S5 B7 S6 B8 S7 B9 S8 S9 WO0 WO1 ST LW PV1",
    "B0 B1 PV2 M MM B2 RV S0 S1 B3 LD OT LN B4 S2 B5 S3 S4 PV0 "
    "S5 B6 S6 LW B7 XN0 XN1 B8 S7 B9 S8 S9 R0 R1 PV1",
    "B0 M B1 MM PV2 S0 B2 S1 B3 RK LD OT S2 S3 LW SC0 B4 B5 PV0 B6 B7 S4 S5 S6 S7 B8 SC1 B9 S8 SC2 S9 PV1 SC3",
]
ORDER_LAST = [
    "S0 S1 B0 B1 M S2 B2 PV2 B3 MM V0 LR LD V1 S3 B4 OT PV0 S4 "
    "XB YT0 S5 B5 YT1 B6 B7 S6 B8 S7 B9 S8 S9 WO0 WO1 PV1 ST LW",
    "B0 B1 M B2 S0 MM DW B3 S1 PV2 RV S2 S3 LN B4 S4 B5 PV0 OT "
    "S5 B6 S6 B7 B8 XN0 XN1 S7 S8 S9 LW B9 R0 PV1 R1",
    "B0 M B1 B2 MM DW PV2 B3 RK B4 OT B5 SC0 B6 SC1 B7 SC2 B8 PV0 LW B9 SC3 PV1",
    "LW TE B0 B1 LT PV2 DW B2 B3 OT B4 B5 PV0 B6 B7 B8 B9 PV1",
]
OF_BEFORE = ("LR", "XB", "YT", "WO", "ST", "RV", "LN", "XN", "R", "RK", "SC")


def items(text, g):
    split = [(word[:-1], int(word[-1])) if word[-1].isdigit() else (word, 0) for word in text.split()]
    return [(name, g, u) for name, u in split]


def steps_of(first, last):
    order = []
    for g, line in enumerate(ORDER_LAST if last else ORDER):
        for name, _, u in items(line, g):
            absent = first and (name in OF_BEFORE + ("V",)
                                or g == 0 and (name in ("OT", "LD") or name == "PV" and u == 2))
            if not absent:
                order.append((name, g, u))
    return order


PROLOGUE = (items("W0 XS W1 Q0 W2 QL0 QS0 C K0 KL0 KS0 PL0 Q1 QL1 QS1 K1 KL1 KS1 PL1 W3 W4 V0 V1 PL2", -3)
            + items("S0 S1 S2 S3 S4 S5 S6 S7 S8 S9", -2) + items("S0 S1 M MM PL3 S2 S3 S4 S5 S6 S7 S8 S9", -1))
EPILOGUE = items("PV2 F00 OT LR DW XB F10 YT0 YT1 F01 WO0 WO1 ST F11 RV LN F21 F02 "
                 "XN0 XN1 F12 R0 R1 F22 RK SC0 SC1 F03 SC2 TL SC3 F13 F23 F04 F14 F24 FE", NG)
SLOTS = 4
UNITS = ("Q", "C", "K", "V", "S", "M", "OT", "YT", "WO", "XN", "R", "RK")


def units_in(order):
    return sum(name in UNITS for name, _, _ in order)


def projected(b, g):
    return b + (g >= 0)


def past(b, g):
    return b + (g == NG)


def tile(pair, odd, k=0):
    return pair + (odd + k) // 2, (odd + k) % 2


def wait(engine, sem, value):
    if not isinstance(value, int) or value > 0:
        engine.wait_ge(sem, value)


class Chain:

    def __init__(self, engine, sem, per_body):
        self.engine, self.sem, self.per_body = engine, sem, per_body
        self.done, self.batch = 0, None

    def link(self, instruction):
        self.done += 1
        instruction.then_inc(self.sem, 1)
        more = 0 if self.batch is None else (self.batch - 1) * self.per_body
        self.engine.wait_ge(self.sem, self.done + more)

    def counted(self, run):
        def counted_run(b, order, const, per):
            in_loop = not isinstance(b, int)
            self.batch, began = (b if in_loop else None), self.done
            run(b, order, const, per)
            if in_loop:
                assert self.done - began == self.per_body, self.done - began
                self.done += (NB - 3) * self.per_body
            self.batch = None
        return counted_run


DVE_LINKS, POOL_LINKS = 28, 1


def kernel_program(nc, x, x_turned, Wq, Wc, Wk, Wv, Wo, bo, router_w, gate_w, up_w, down_w, out):
    tokens = x.rearrange("b (t p) c -> p (b t) c", p=P)
    channels = x_turned.rearrange("b (k p) t -> p b k t", p=P)
    out_rows = out.rearrange("b t c -> (b t) c")
    first_body, middle_body, last_body = steps_of(True, False), steps_of(False, False), steps_of(False, True)
    U_MID = units_in(middle_body)
    U_START = units_in(PROLOGUE) + units_in(first_body)
    U0 = -U_START % SLOTS
    assert U_MID % SLOTS == 0

    def bodies(run, fori):
        run(0, first_body, U0 + units_in(PROLOGUE), 0)
        with fori(1, NB - 1) as b:
            run(b, middle_body, U0 + U_START - U_MID, U_MID)
        run(NB - 1, last_body, U0 + U_START + (NB - 2) * U_MID, 0)

    U_END = U0 + U_START + (NB - 2) * U_MID + units_in(last_body)
    EPILOGUE_UNITS = [n for n in range(U_END, U_END + SLOTS * len(EPILOGUE)) if n % SLOTS < 2]

    def numbered(order, const):
        units = units_in(order)
        numbers = EPILOGUE_UNITS[:units] if order is EPILOGUE else list(range(const, const + units))
        done = (U_END if order is EPILOGUE else const) - U0
        unit = None
        for name, g, u in order:
            if name in UNITS:
                unit, done = numbers.pop(0), done + 1
            yield name, g, u, unit, done

    qk_dram = nc.dram_tensor("qk_parts", [NB, 2, 3, C, T], BF16, kind="Internal").ap()
    max_dram = nc.dram_tensor("maxima", [NB * NG, 3 * GH * TT, P], BF16, kind="Internal").ap()
    rows_dram = nc.dram_tensor("expert_rows", [NE * REGION + P, ROW], F32, kind="Internal").ap()

    ctx = ExitStack()
    with ctx:
        def sb(name, shape, dt=F32):
            return ctx.enter_context(nc.sbuf_tensor(name, shape, dt))

        def sem(name):
            return ctx.enter_context(nc.semaphore(name))

        wq = sb("wq", [P, 2, CC, C])
        wc = sb("wc", [P, 2, CC, LAT])
        wk = sb("wk", [P, 2, 1, C])
        wv = sb("wv", [P, 2, 1, C])
        wo = sb("wo", [P, 2, CC, C])
        wr = sb("wr", [P, CC, NE])
        bias = sb("bias", [P, C])
        gate = sb("gate", [P, NE, CC, NI])
        up = sb("up", [P, NE, CC, NI])
        down = sb("down", [P, NE, IC, C])
        stacks = down[:, :, :, :].rearrange("p e i c -> p (e i c)").bitcast(BF16)
        q_stack = stacks[:, 0:NH * T].rearrange("p (h t) -> p h t", h=NH)
        k_stack = stacks[:, NH * T:2 * NH * T].rearrange("p (h t) -> p h t", h=NH)
        ident = sb("ident", [P, P])
        ident_b = sb("ident_b", [P, P], BF16)
        causal = sb("causal", [P, P], BF16)
        earlier = sb("earlier", [P, P], BF16)
        ones_b = sb("ones_b", [P, P], BF16)
        expert8 = sb("expert8", [P, NE])
        tile_no = sb("tile_no", [P, NT])
        minus_half = sb("minus_half", [P, TT])
        padding = sb("padding", [P, ROW])
        x_in = sb("x_in", [P, CC, T])
        xT = sb("xT", [P, 2, CC, T])
        cT = sb("cT", [P, 2, 1, T])
        parts = [[sb(f"part{i}{s}", [P, CC, T], BF16) for s in range(3)] for i in range(2)]
        rest = sb("rest", [P, CC, T])
        vv = sb("vv", [P, TT, NH * VW + HS - 1])
        row_max = sb("row_max", [P, GH, TT])
        max_parts = sb("max_parts", [P, 3, GH, TT], BF16)
        max_rest = sb("max_rest", [P, GH, TT])
        maxT = sb("maxT", [3 * GH * TT, P], BF16)
        probs = sb("probs", [P, BANKS, T])
        projections = ((wq, Wq), (wc, Wc), (wk, Wk), (wv, Wv), (wo, Wo))
        before_probs = probs[:, :, :].rearrange("p k t -> p (k t)")
        raw, column = [], 0
        for w, _ in projections:
            k, n = w.shape[2:]
            raw.append(before_probs[:, column:column + k * n].rearrange("p (k n) -> p k n", k=k))
            column += k * n
        oT = sb("oT", [P, 2, T])
        rsum = sb("rsum", [P, 2, TT, GH])
        y = sb("y", [P, TT, C])
        yT = sb("yT", [P, 2, CC, T])
        xr = sb("xr", [P, TT, ROW])
        stats = sb("stats", [P, TT, 6])
        mean_var = sb("mean_var", [P, TT, 2])
        rstd = sb("rstd", [P, TT])
        x1T = sb("x1T", [P, CC, T])
        route = sb("route", [P, TT, NE])
        pick = sb("pick", [P, TT, NE])
        pick_min = sb("pick_min", [P, TT])
        onehot = sb("onehot", [P, TT, NE], BF16)
        next_row = sb("next_row", [P, NE])
        region0 = sb("region0", [P, NE])
        place = sb("place", [P, TT, NE])
        dest = sb("dest", [P, TT])
        dest_i = sb("dest_i", [P, TT], I32)
        token_no = sb("token_no", [P, TT])
        t8 = sb("t8", [P, 5, NE])
        early_of = sb("early_of", [P, NE])
        t8i = sb("t8i", [P, NE], I32)
        one8 = sb("one8", [P, NE])
        sel = sb("sel", [P, 2, NT, NE])
        tab = sb("tab", [P, 4, NT])
        row_tab = sb("row_tab", [P, NT], I32)
        expert_tab = sb("expert_tab", [P, NT], I32)
        pad_tab = sb("pad_tab", [P, NE], I32)
        xs = sb("xs", [P, 2, ROW])
        kept = sb("kept", [P, 2, ROW])
        tile_buffers, column = [], 0
        for n in (CC * P, NI, NI, NI, C):
            tile_buffers.append(before_probs[:, column:column + 2 * n].rearrange("p (o n) -> p o n", o=2))
            column += 2 * n
        xsT, silu, hh, hT, z = tile_buffers
        zstats = sb("zstats", [P, 2, 6])
        zmv = sb("zmv", [P, 2, 2])
        zrstd = sb("zrstd", [P, 2])
        zi = sb("zi", [P, 2], I32)

        pa = ctx.enter_context(nc.psum_tensor("pa", [P, SLOTS, T], F32))
        pb = ctx.enter_context(nc.psum_tensor("pb", [P, 2, T], F32))
        pv = ctx.enter_context(nc.psum_tensor("pv", [P, 2, T], F32))

        y2 = pb[:, 1, 0:C]

        const_done = sem("const_done")
        ones_done = sem("ones_done")
        vv_ones = sem("vv_ones")
        stack_ones = sem("stack_ones")
        raw_in = [sem("w%s_in" % name) for name in "qckvo"]
        weights_in = sem("weights_in")
        high_weights = sem("high_weights")
        weights_split = sem("weights_split")
        xT_high, xT_low, cT_high, yT_high = sem("xT_high"), sem("xT_low"), sem("cT_high"), sem("yT_high")
        gate_up_in = sem("gate_up_in")
        down_in = sem("down_in")
        xT_in = sem("xT_in")
        xr_in = sem("xr_in")
        unit_ready = sem("unit_ready")
        unit_read = [sem(f"unit{k}_read") for k in range(SLOTS)]
        high_ready = [sem(f"high_ready{m}") for m in range(CC)]
        mid_ready = [sem(f"mid_ready{m}") for m in range(CC)]
        low_ready = [sem(f"low_ready{m}") for m in range(CC)]
        parts_out = [sem(f"parts_out{m}") for m in range(CC)]
        stack_in = [sem(f"stack_in{g}") for g in range(NG)]
        max_parts_ready = sem("max_parts_ready")
        max_out = sem("max_out")
        max_in = [sem("max_in0"), sem("max_in1")]
        scores_ready = sem("scores_ready")
        exp_done = sem("exp_done")
        masked = sem("masked")
        pv_done = sem("pv_done")
        oT_ready = sem("oT_ready")
        xr_biased = sem("xr_biased")
        var_ready = sem("var_ready")
        rstd_ready = sem("rstd_ready")
        x1_ready = sem("x1_ready")
        onehot_ready = sem("onehot_ready")
        dest_ready = sem("dest_ready")
        scattered = sem("scattered")
        ends_ready = sem("ends_ready")
        tables_ready = sem("tables_ready")
        pads_out = sem("pads_out")
        dve_chain = sem("dve_chain")
        pool_chain = sem("pool_chain")
        xs_in = [sem("xs_in0"), sem("xs_in1")]
        rows_kept = sem("rows_kept")
        xsT_psum = sem("xsT_psum")
        xsT_ready = sem("xsT_ready")
        gate_ready = sem("gate_ready")
        up_ready = sem("up_ready")
        silu_done = sem("silu_done")
        h_ready = sem("h_ready")
        hT_psum = sem("hT_psum")
        hT_ready = sem("hT_ready")
        y2_ready = sem("y2_ready")
        z_ready = sem("z_ready")
        zvar_ready = sem("zvar_ready")
        zrstd_ready = sem("zrstd_ready")
        zstats_ready = sem("zstats_ready")
        zeps_ready = sem("zeps_ready")
        z_normed = sem("z_normed")
        out_done = [sem("out_done0"), sem("out_done1")]

        def slot(idx):
            return idx % SLOTS

        def earlier_units(n):
            return n // SLOTS - (n % SLOTS < U0)

        def wait_read(engine, n, b, per):
            engine.wait_ge(unit_read[slot(n)], earlier_units(n) + 1 + b * (per // SLOTS))

        def wait_bank(pe, n, b, per):
            wait(pe, unit_read[slot(n)], earlier_units(n) + b * (per // SLOTS))

        def apart(engine):
            engine.nop(nofuse=True)

        block = ctx.enter_context(nc.Block())

        @block.sync
        def _(sp):
            sp.dma_start(x_in[:], channels[:, 0]).then_inc(xT_in, 16)
            for k in (1, 3, 4):
                sp.dma_start(raw[k], projections[k][1].rearrange("(k p) n -> p k n", p=P)).then_inc(raw_in[k], 16)
            sp.dma_start(wr[:], router_w.rearrange("(k p) n -> p k n", p=P)).then_inc(weights_in, 16)
            sp.dma_start(bias[:], bo.rearrange("(o n) -> o n", o=1).to_broadcast([P, C])).then_inc(weights_in, 16)

            def spill_parts(i, m, bn):
                for s, made in ((0, high_ready[m]), (1, mid_ready[m]), (2, low_ready[m])):
                    sp.wait_ge(made, bn * 2 + i + 1)
                    apart(sp)
                    dst = qk_dram[bass.ds(bn, 1), i, s, m * P:(m + 1) * P, :].rearrange("o p t -> (o p) t")
                    sp.dma_start(dst, parts[i][s][:, m, :]).then_inc(parts_out[m], 16)

            def load_stacks(bn, g):
                for i, stack in enumerate((q_stack, k_stack)):
                    row = 0
                    for r, terms in enumerate(RUNS):
                        s0, s1 = (r, r + 1) if i == 0 else (0, terms)
                        src = qk_dram[bass.ds(bn, 1), i, s0:s1, g * GH * HS:(g + 1) * GH * HS, :]
                        src = src.rearrange("o s (d h) t -> (o s) d (h t)", d=HS)
                        if i == 0:
                            src = src.to_broadcast([terms, HS, GH * T])
                        sp.dma_start(stack[row:row + terms * HS, g * GH:(g + 1) * GH, :].rearrange("k h t -> k (h t)"), src)\
                            .then_inc(stack_in[g], 16)
                        row += terms * HS

            def move_maxima(b, g, unit, per):
                G = b * NG + g
                wait_read(sp, unit, b, per)
                sp.dma_start(max_dram[bass.ds(G, 1)].rearrange("o r p -> (o r) p"), maxT[:]).then_inc(max_out, 16)
                sp.wait_ge(max_out, G * 16 + 16)
                g4 = g % NG
                src = max_dram[bass.ds(G, 1)].rearrange("o (s r) p -> (o s) (r p)", s=3)
                dst = q_stack[KS:KM, g4 * GH:(g4 + 1) * GH, :].rearrange("s h t -> s (h t)")
                sp.dma_start(dst, src).then_inc(max_in[g % 2], 16)

            def load_down(g):
                sp.wait_ge(scores_ready, ((NB - 1) * NG + g + 1) * BANKS)
                for e in (g, NG + g):
                    sp.dma_start(down[:, e], down_w[e].rearrange("(k p) n -> p k n", p=P)).then_inc(down_in, 16)

            def load_tile(pair, odd):
                i = 2 * pair + odd
                row = sp.value_load(row_tab[0:1, bass.ds(i, 1)], min_val=0, max_val=PAD_ROW)
                wait(sp, xsT_psum, i - 1)
                wait(sp, rows_kept, i - 1)
                sp.dma_start(xs[:, odd, :], rows_dram[bass.ds(row, P), :]).then_inc(xs_in[odd], 16)

            def run(b, order, const, per):
                for name, g, u, unit, _ in numbered(order, const):
                    if name == "M":
                        maxima = unit
                    if name == "LX":
                        sp.wait_ge(xT_high, b + 1)
                        apart(sp)
                        sp.wait_ge(xT_low, b + 1)
                        apart(sp)
                        sp.dma_start(x_in[:], channels[:, bass.ds(b + 1, 1)].rearrange("p o k t -> p (o k) t"))\
                            .then_inc(xT_in, 16)
                    elif name in ("QS", "KS"):
                        spill_parts(int(name == "KS"), u, projected(b, g))
                    elif name == "PL":
                        sp.wait_ge(parts_out[u // (NG // CC)], 6 * 16)
                        load_stacks(0, u)
                    elif name == "MM":
                        move_maxima(b, g + 1, maxima, per)
                    elif name == "LD":
                        sp.wait_ge(parts_out[(g - 1) % NG // (NG // CC)], (b + (g > 0)) * 96 + 96)
                        apart(sp)
                        sp.wait_ge(scores_ready, (b * NG + g) * BANKS)
                        apart(sp)
                        load_stacks(b + (g > 0), (g - 1) % NG)
                    elif name == "DW":
                        load_down(g - 1)
                    elif name == "LT":
                        sp.wait_ge(tables_ready, 1)
                        sp.wait_ge(scattered, (NB - 1) * 64)
                        for i in range(2):
                            load_tile(0, i)
                    elif name == "F1" and u + 2 < EARLY:
                        load_tile(*tile(0, 0, u + 2))
                    elif name == "LR":
                        wait(sp, scattered, (past(b, g) - 1) * 64)
                        apart(sp)
                        sp.dma_start(xr[:, :, 0:C], tokens[:, bass.ds((past(b, g) - 1) * TT, TT), :]).then_inc(xr_in, 16)
                    elif name == "LW":
                        e, dst, w = b * 2 + g // 2, (gate, up)[g % 2], (gate_w, up_w)[g % 2]
                        sp.dma_start(dst[:, bass.ds(e, 1)].rearrange("p o k n -> p (o k) n"),
                                     w[bass.ds(e, 1)].rearrange("o (k p) n -> p (o k) n", p=P)).then_inc(gate_up_in, 16)

            run(0, PROLOGUE, U0, 0)
            bodies(run, sp.Fori)
            run(NB - 1, EPILOGUE, U_END, 0)

            sp.dma_start(rows_dram[PAD_ROW:PAD_ROW + P, :], padding[:]).then_inc(pads_out, 16)
            sp.wait_ge(ends_ready, 1)
            for e in range(NE):
                row = sp.value_load(pad_tab[0:1, e:e + 1], min_val=e * REGION, max_val=(e + 1) * REGION - P)
                sp.dma_start(rows_dram[bass.ds(row, P), :], padding[:]).then_inc(pads_out, 16)
            sp.wait_ge(tables_ready, 2)
            sp.wait_ge(pads_out, (NE + 1) * 16)
            sp.wait_ge(scattered, NB * 64)
            load_tile(*tile(0, 0, EARLY))
            load_tile(*tile(0, 0, EARLY + 1))
            with sp.Fori(EARLY // 2 + 1, NT // 2) as p:
                load_tile(p, 1)
                load_tile(p + 1, 0)
            sp.wait_ge(out_done[0], (NT + 1) // 2 * 16)
            sp.wait_ge(out_done[1], NT // 2 * 16)

        @block.tensor
        def _(pe):
            pe.wait_ge(const_done, 1)

            def exact(dst, stationary, moving, chunks):
                terms = [(i, j, c) for c in range(chunks) for i, j in ((0, 0), (0, 1), (1, 0))]
                for i, j, c in terms:
                    last = nc.tensor.matmul(dst, stationary[:, i, c, :].bitcast(F32R), moving[:, j, c, :].bitcast(F32R),
                                            start=(i, j, c) == terms[0], stop=(i, j, c) == terms[-1])
                return last

            def expert_of(i):
                return pe.value_load(expert_tab[0:1, bass.ds(i, 1)], min_val=0, max_val=NE - 1)

            def turn_rows(pair, odd):
                i = 2 * pair + odd
                pe.wait_ge(xs_in[odd], pair * 16 + 16)
                wait(pe, xsT_ready, i)
                for c in range(CC):
                    last = nc.tensor.transpose(pv[:, 0, c * P:(c + 1) * P], xs[:, odd, c * P:(c + 1) * P], ident[:])
                last.then_inc(xsT_psum, 1)

            def times(dst, rows, weights, expert, chunks):
                for c in range(chunks):
                    last = nc.tensor.matmul(dst, rows[:, c * P:(c + 1) * P],
                                            weights[:, bass.ds(expert, 1), c, :].rearrange("p o n -> p (o n)"),
                                            start=(c == 0), stop=(c == chunks - 1))
                return last

            def turn_inner(pair, odd):
                i = 2 * pair + odd
                pe.wait_ge(h_ready, i + 1)
                wait(pe, hT_ready, i)
                for c in range(IC):
                    last = nc.tensor.transpose(pb[:, 0, c * P:(c + 1) * P], hh[:, odd, c * P:(c + 1) * P], ident[:])
                last.then_inc(hT_psum, 1)

            def down_of(pair, odd):
                i = 2 * pair + odd
                expert = expert_of(i)
                pe.wait_ge(hT_ready, i + 1)
                wait(pe, z_ready, i)
                times(y2, hT[:, odd, :], down, expert, IC).then_inc(y2_ready, 1)

            def first_step(pair, odd, follows=True):
                i = 2 * pair + odd
                expert = expert_of(i)
                pe.wait_ge(xsT_ready, i + 1)
                wait(pe, silu_done, i)
                times(pa[:, 2, :], xsT[:, odd, :], gate, expert, CC).then_inc(gate_ready, 1)
                if follows:
                    turn_inner(*tile(pair, odd, -1))

            def second_step(pair, odd, more=True):
                i = 2 * pair + odd
                expert = expert_of(i)
                wait(pe, h_ready, i)
                times(pa[:, 3, :], xsT[:, odd, :], up, expert, CC).then_inc(up_ready, 1)
                if more:
                    turn_rows(*tile(pair, odd, 1))

            def third_step(pair, odd):
                down_of(*tile(pair, odd, -1))

            def run(b, order, const, per):
                unit = {}
                first = order is first_body
                for name, g, u, number, _ in numbered(order, const):
                    G = b * NG + g
                    if name in UNITS:
                        s = slot(number)
                        wait_bank(pe, number, b, per)
                        if name in ("K", "V", "YT", "WO", "R"):
                            apart(pe)
                        unit[name, u] = number
                    if order is PROLOGUE and name in ("Q", "C", "K", "V"):
                        pe.wait_ge(weights_split, {"Q": 1, "C": 2, "K": 3, "V": 5}[name])
                    if order is PROLOGUE and name == "V":
                        pe.wait_ge(weights_in, 2 * 16)
                    if name in ("Q", "C"):
                        pe.wait_ge(xT_high, projected(b, g) + 1)
                        apart(pe)
                        pe.wait_ge(xT_low, projected(b, g) + 1)
                        apart(pe)
                    if name == "Q":
                        last = exact(pa[:, s, :], wq[:, :, :, u * P:(u + 1) * P], xT, CC)
                    elif name == "C":
                        last = exact(pa[:, s, :], wc, xT, CC)
                    elif name == "K":
                        wait_read(pe, unit["C", 0], b, per)
                        last = exact(pa[:, s, :], wk[:, :, :, u * P:(u + 1) * P], cT, 1)
                    elif name == "V":
                        if order is PROLOGUE and u == 0:
                            wait_read(pe, unit["C", 0], b, per)
                        for t in range(2):
                            tt = 2 * u + t
                            last = exact(pa[:, s, t * C:(t + 1) * C], cT[:, :, :, tt * P:(tt + 1) * P], wv, 1)
                    elif name == "S":
                        g4 = (g + 2) % NG
                        if u == 0:
                            bs = b if g + 2 < NG else b + 1
                            pe.wait_ge(stack_in[g4], (bs + 1) * 2 * len(RUNS) * 16)

                        def scores(dst, h, qt):
                            hh_ = g4 * GH + h
                            w = (qt + 1) * P
                            nc.tensor.matmul(dst[:, 0:w], q_stack[0:KS, hh_, qt * P:w], k_stack[0:KS, hh_, 0:w],
                                             start=True, stop=False)
                            return nc.tensor.matmul(dst[:, qt * P:w], ident_b[:], causal[:], start=False, stop=True)

                        if u < 2:
                            for j in range(2):
                                last = scores(pa[:, s, j * 2 * P:(j + 1) * 2 * P], 2 * u + j, 1)
                        elif u < 6:
                            scores(pa[:, s, 0:3 * P], u - 2, 2)
                            last = scores(pa[:, s, 3 * P:T], u - 2, 0)
                        else:
                            last = scores(pa[:, s, :], u - 6, 3)
                    elif name == "M":
                        pe.wait_ge(max_parts_ready, G + 2)
                        apart(pe)
                        last = nc.tensor.transpose(pa[0:3 * GH * TT, s, 0:P // 2].bitcast(BF16),
                                                   max_parts[:, :, :, :].rearrange("p s h t -> p (s h t)"), ident_b[:])
                    elif name == "B":
                        if u == 0 and first and g == 0:
                            pe.wait_ge(stack_ones, 1)
                        if u == 0:
                            pe.wait_ge(max_in[g % 2], b * 32 + g // 2 * 16 + 16)
                        wait(pe, exp_done, G * BANKS + u - 1)

                        def turned(h, kt, col):
                            hh_ = g * GH + h
                            w = T - kt * P
                            return nc.tensor.matmul(pb[:, u % 2, col:col + w], k_stack[0:KM, hh_, kt * P:(kt + 1) * P],
                                                    q_stack[0:KM, hh_, kt * P:T], start=True, stop=True)

                        if u < 4:
                            last = turned(u, 0, 0)
                        elif u < 8:
                            turned(u - 4, 1, 0)
                            last = turned(u - 4, 3, 3 * P)
                        else:
                            for j in range(2):
                                last = turned(2 * (u - 8) + j, 2, j * 2 * P)
                        last.then_inc(scores_ready, 1)
                    elif name == "PV":
                        if u == 2:
                            G = G - 1
                        bank = (g - (u == 2)) % 2
                        g4 = (g - (u == 2)) % NG
                        if u == 0:
                            wait(pe, oT_ready, G - 1)
                        if u == 0 and g == 0 and ("V", 1) in unit:
                            wait_read(pe, unit["V", 0], b, per)
                            apart(pe)
                            wait_read(pe, unit["V", 1], b, per)
                        pe.wait_ge(masked, G * 3 + u + 1)
                        for kt in ((0,), (1, 3), (2,))[u]:
                            for h in range(GH):
                                hh_ = g4 * GH + h
                                if kt == 0:
                                    moving = probs[:, h, :]
                                elif kt == 2:
                                    moving = probs[:, 8 + h // 2, h % 2 * 2 * P:(h % 2 + 1) * 2 * P]
                                else:
                                    moving = probs[:, 4 + h, 0:3 * P] if kt == 1 else probs[:, 4 + h, 3 * P:T]
                                last = nc.tensor.matmul(pv[32 * h:32 * h + 32, bank, kt * P:T],
                                                        vv[:, kt, hh_ * VW:hh_ * VW + 32], moving,
                                                        start=(kt == 0), stop=(kt == 2))
                        last.then_inc(pv_done, 1)
                    elif name == "OT":
                        pe.wait_ge(oT_ready, G)
                        for t in range(TT):
                            last = nc.tensor.transpose(pa[:, s, t * P:(t + 1) * P],
                                                       oT[:, (g - 1) % 2, t * P:(t + 1) * P], ident[:])
                    elif name == "YT":
                        wait_read(pe, unit["OT", 0], b, per)
                        for t in range(TT):
                            last = nc.tensor.transpose(pa[:, s, t * P:(t + 1) * P], y[:, t, u * P:(u + 1) * P], ident[:])
                    elif name == "WO":
                        wait_read(pe, unit["YT", 0], b, per)
                        apart(pe)
                        wait_read(pe, unit["YT", 1], b, per)
                        for t in range(2):
                            tt = 2 * u + t
                            last = exact(pa[:, s, t * C:(t + 1) * C], yT[:, :, :, tt * P:(tt + 1) * P], wo, CC)
                    elif name == "XN":
                        pe.wait_ge(x1_ready, past(b, g))
                        for t in range(TT):
                            last = nc.tensor.transpose(pa[:, s, t * P:(t + 1) * P], xr[:, t, u * P:(u + 1) * P], ident[:])
                    elif name == "R":
                        wait_read(pe, unit["XN", 0], b, per)
                        apart(pe)
                        wait_read(pe, unit["XN", 1], b, per)
                        for t in range(2):
                            for c in range(CC):
                                tt = 2 * u + t
                                last = nc.tensor.matmul(pa[:, s, t * NE:(t + 1) * NE], x1T[:, c, tt * P:(tt + 1) * P],
                                                        wr[:, c, :], start=(c == 0), stop=(c == CC - 1))
                    elif name == "RK":
                        pe.wait_ge(onehot_ready, past(b, g))
                        for t in range(TT + 1):
                            dst = pa[:, s, t * NE:(t + 1) * NE]
                            for t2 in range(min(t, TT)):
                                last = nc.tensor.matmul(dst, ones_b[:], onehot[:, t2, :], start=(t2 == 0),
                                                        stop=(t == TT and t2 == TT - 1))
                            if t < TT:
                                last = nc.tensor.matmul(dst, earlier[:], onehot[:, t, :], start=(t == 0), stop=True)
                    elif name == "F0":
                        if u == 0:
                            pe.wait_ge(oT_ready, NB * NG - 1)
                            pe.wait_ge(exp_done, NB * NG * BANKS)
                            for n in range(U_END - SLOTS, U_END):
                                if slot(n) >= 2:
                                    wait_read(pe, n, 0, 0)
                            pe.wait_ge(gate_up_in, 2 * NE * 16)
                            pe.wait_ge(tables_ready, 1)
                            turn_rows(0, 0)
                        first_step(*tile(0, 0, u), follows=u > 0)
                    elif name == "F1":
                        second_step(*tile(0, 0, u), more=u < EARLY - 1)
                    elif name == "F2":
                        if u == 1:
                            pe.wait_ge(down_in, NE * 16)
                        third_step(*tile(0, 0, u))
                    elif name == "FE":
                        turn_inner(*tile(0, 0, EARLY - 1))
                        down_of(*tile(0, 0, EARLY - 1))
                    if name in UNITS:
                        last.then_inc(unit_ready, 1)

            run(0, PROLOGUE, U0, 0)
            bodies(run, pe.Fori)
            run(NB - 1, EPILOGUE, U_END, 0)

            pe.wait_ge(tables_ready, 2)
            turn_rows(*tile(0, 0, EARLY))
            first_step(*tile(0, 0, EARLY), follows=False)
            second_step(*tile(0, 0, EARLY))
            first_step(*tile(0, 0, EARLY + 1))
            second_step(*tile(0, 0, EARLY + 1))
            third_step(*tile(0, 0, EARLY + 1))
            with pe.Fori(EARLY // 2 + 1, NT // 2 - 1) as p:
                for k in range(2):
                    first_step(*tile(p, 1, k))
                    second_step(*tile(p, 1, k))
                    third_step(*tile(p, 1, k))
            first_step(NT // 2 - 1, 1)
            second_step(NT // 2 - 1, 1)
            third_step(NT // 2 - 1, 1)
            first_step(NT // 2, 0)
            second_step(NT // 2, 0, more=False)
            third_step(NT // 2, 0)
            turn_inner(NT // 2, 0)
            down_of(NT // 2, 0)

        @block.scalar
        def _(act):
            for k in (0, 2):
                act.dma_start(raw[k], projections[k][1].rearrange("(k p) n -> p k n", p=P)).then_inc(raw_in[k], 16)
            nc.scalar.preload_act_table(ACT.Exp)
            act.wait_ge(vv_ones, 1)

            def rows_turned(pair, odd):
                i = 2 * pair + odd
                act.wait_ge(xsT_psum, i + 1)
                wait(act, up_ready, i - 1)
                nc.scalar.activation(xsT[:, odd, :], pv[:, 0, 0:CC * P], ACT.Copy).then_inc(xsT_ready, 1)

            def inner_turned(pair, odd):
                i = 2 * pair + odd
                act.wait_ge(hT_psum, i + 1)
                wait(act, y2_ready, i - 1)
                nc.scalar.activation(hT[:, odd, :], pb[:, 0, :], ACT.Copy).then_inc(hT_ready, 1)

            def first_step(pair, odd, follows=True):
                i = 2 * pair + odd
                act.wait_ge(gate_ready, i + 1)
                wait(act, h_ready, i - 1)
                nc.scalar.activation(silu[:, odd, :], pa[:, 2, :], ACT.Silu).then_inc(silu_done, 1)
                if follows:
                    inner_turned(*tile(pair, odd, -1))

            def run(b, order, const, per):
                for name, g, u, unit, units_ready in numbered(order, const):
                    G = b * NG + g
                    s = slot(unit or 0)
                    ready = units_ready + b * per
                    if name == "XS":
                        act.wait_ge(xT_in, projected(b, g) * 16 + 16)
                        nc.scalar.activation(xT[:, 0].bitcast(F32R), x_in[:], ACT.Copy).then_inc(xT_high, 1)
                    elif name in ("Q", "K"):
                        i = int(name == "K")
                        act.wait_ge(unit_ready, ready)
                        wait(act, parts_out[u], projected(b, g) * 96)
                        nc.scalar.activation(parts[i][0][:, u, :], pa[:, s, :], ACT.Copy).then_inc(high_ready[u], 1)
                    elif name == "C":
                        act.wait_ge(unit_ready, ready)
                        nc.scalar.activation(cT[:, 0, 0].bitcast(F32R), pa[:, s, :], ACT.Copy).then_inc(cT_high, 1)
                    elif name == "V":
                        act.wait_ge(unit_ready, ready)
                        v4 = vv[:, :, 0:NH * VW].rearrange("p t (h d) -> p t h d", d=VW)
                        for t in range(2):
                            last = nc.scalar.activation(v4[:, 2 * u + t, :, 0:HS], pa[:, s, t * C:(t + 1) * C]
                                                        .rearrange("p (h d) -> p h d", d=HS), ACT.Copy)
                        last.then_inc(unit_read[s], 1)
                    elif name == "B":
                        act.wait_ge(scores_ready, G * BANKS + u + 1)
                        wait(act, pv_done, (G - 1) * 3 + (1 if u < 4 else 2 if u < 8 else 3))
                        nc.scalar.activation(probs[:, u, :], pb[:, u % 2, :], ACT.Exp, scale=SCORE_SCALE)\
                            .then_inc(exp_done, 1)
                    elif name == "PV" and u == 2:
                        act.wait_ge(pv_done, G * 3)
                        nc.scalar.activation(oT[:, (g - 1) % 2, :], pv[:, (g - 1) % 2, :], ACT.Copy)\
                            .then_inc(oT_ready, 1)
                    elif name == "M":
                        act.wait_ge(unit_ready, ready)
                        wait(act, max_out, (G + 1) * 16)
                        nc.scalar.activation(maxT[:], pa[0:3 * GH * TT, s, 0:P // 2].bitcast(BF16), ACT.Copy)\
                            .then_inc(unit_read[s], 1)
                    elif name == "YT":
                        act.wait_ge(unit_ready, ready)
                        nc.scalar.activation(yT[:, 0, u].bitcast(F32R), pa[:, s, :], ACT.Copy).then_inc(yT_high, 1)
                    elif name == "XN":
                        act.wait_ge(unit_ready, ready)
                        nc.scalar.activation(x1T[:, u, :], pa[:, s, :], ACT.Copy)\
                            .then_inc(unit_read[s], 1)
                    elif name == "R":
                        act.wait_ge(unit_ready, ready)
                        nc.scalar.activation(route[:, 2 * u:2 * u + 2, :].rearrange("p t e -> p (t e)"), pa[:, s, 0:2 * NE],
                                             ACT.Exp, scale=-1.0)\
                            .then_inc(unit_read[s], 1)
                    elif name == "F0":
                        if u == 0:
                            rows_turned(0, 0)
                        first_step(*tile(0, 0, u), follows=u > 0)
                    elif name == "F1" and u < EARLY - 1:
                        rows_turned(*tile(0, 0, u + 1))
                    elif name == "FE":
                        inner_turned(*tile(0, 0, EARLY - 1))

            run(0, PROLOGUE, U0, 0)
            bodies(run, act.Fori)
            run(NB - 1, EPILOGUE, U_END, 0)

            rows_turned(*tile(0, 0, EARLY))
            first_step(*tile(0, 0, EARLY), follows=False)
            rows_turned(*tile(0, 0, EARLY + 1))
            first_step(*tile(0, 0, EARLY + 1))
            rows_turned(*tile(0, 0, EARLY + 2))
            with act.Fori(EARLY // 2 + 1, NT // 2 - 1) as p:
                for k in range(2):
                    first_step(*tile(p, 1, k))
                    rows_turned(*tile(p, 1, k + 1))
            first_step(NT // 2 - 1, 1)
            rows_turned(NT // 2, 0)
            first_step(NT // 2, 0)
            inner_turned(NT // 2, 0)

        @block.vector
        def _(dve):
            chain = Chain(dve, dve_chain, DVE_LINKS)
            V = nc.vector

            def inner(pair, odd):
                i = 2 * pair + odd
                dve.wait_ge(silu_done, i + 1)
                dve.wait_ge(up_ready, i + 1)
                wait(dve, hT_psum, i - 1)
                V.tensor_tensor(hh[:, odd, :], pa[:, 3, :], silu[:, odd, :], ALU.mult).then_inc(h_ready, 1)

            def keep(pair, odd):
                dve.wait_ge(xs_in[odd], pair * 16 + 16)
                apart(dve)
                V.tensor_copy(kept[:, odd, :], xs[:, odd, :]).then_inc(rows_kept, 1)

            def outer(pair, odd):
                i = 2 * pair + odd
                dve.wait_ge(y2_ready, i + 1)
                dve.wait_ge(rows_kept, i + 1)
                wait(dve, out_done[odd], pair * 16)
                V.scalar_tensor_tensor(z[:, odd, :], y2, kept[:, odd, C:C + 1], kept[:, odd, 0:C],
                                       ALU.mult, ALU.add).then_inc(z_ready, 1)
                V.tensor_copy(zi[:, odd:odd + 1], kept[:, odd, C + 1:C + 2])
                dve.wait_ge(z_ready, i + 1)
                V.bn_stats(zstats[:, odd, :], z[:, odd, :]).then_inc(zstats_ready, 1)
                dve.wait_ge(zstats_ready, i + 1)
                apart(dve)
                V.bn_aggr(zmv[:, odd, :], zstats[:, odd, :]).then_inc(zvar_ready, 1)

            def norm(pair, odd):
                i = 2 * pair + odd
                dve.wait_ge(zrstd_ready, i + 1)
                V.tensor_scalar(z[:, odd, :], z[:, odd, :], zmv[:, odd, 0:1], zrstd[:, odd:odd + 1],
                                ALU.subtract, ALU.mult).then_inc(z_normed, 1)

            def first_step(pair, odd, outer_too=True):
                if outer_too:
                    outer(*tile(pair, odd, -2))
                keep(pair, odd)

            def second_step(pair, odd, norm_too=True):
                inner(pair, odd)
                if norm_too:
                    norm(*tile(pair, odd, -2))

            def make_tables(early):
                t0, t1 = (0, EARLY) if early else (EARLY, NT)
                n = t1 - t0
                rows, tiles, upto, before, start = (t8[:, k, :] for k in range(5))
                chain.link(V.tensor_tensor(rows, next_row[:], region0[:], ALU.subtract))
                if not early:
                    chain.link(V.tensor_scalar(rows, rows, float(P - 1), None, ALU.add))
                chain.link(V.tensor_copy(t8i[:], rows))
                chain.link(V.tensor_single_scalar(t8i[:], t8i[:], 7, ALU.arith_shift_right))
                chain.link(V.tensor_copy(tiles, t8i[:]))
                if early:
                    chain.link(V.tensor_copy(start, region0[:]))
                else:
                    chain.link(V.tensor_tensor(tiles, tiles, early_of[:], ALU.subtract))
                    chain.link(V.scalar_tensor_tensor(start, early_of[:], float(P), region0[:], ALU.mult, ALU.add))
                chain.link(V.tensor_tensor_scan(upto, one8[:], tiles, 0.0, ALU.mult, ALU.add))
                chain.link(V.tensor_tensor(before, upto, tiles, ALU.subtract))

                def by_tile(a):
                    return a.rearrange("p (o e) -> p o e", o=1).to_broadcast([P, n, NE])

                no = tile_no[:, 0:n].rearrange("p (t o) -> p t o", o=1).to_broadcast([P, n, NE])
                s0, s1 = sel[:, 0, 0:n], sel[:, 1, 0:n]
                chain.link(V.tensor_tensor(s0, no, by_tile(before), ALU.is_ge))
                chain.link(V.tensor_tensor(s1, no, by_tile(upto), ALU.is_lt))
                chain.link(V.tensor_tensor(s0, s0, s1, ALU.mult))
                if early:
                    chain.link(V.tensor_reduce(early_of[:], s0.rearrange("p t e -> p e t"), AX.X, ALU.add))
                chain.link(V.scalar_tensor_tensor(before, before, -float(P), start, ALU.mult, ALU.add))
                chain.link(V.tensor_tensor(s1, s0, by_tile(before), ALU.mult))
                base, used, away, number = (tab[:, k, 0:n] for k in range(4))
                chain.link(V.tensor_reduce(base, s1, AX.X, ALU.add))
                chain.link(V.tensor_reduce(used, s0, AX.X, ALU.add))
                chain.link(V.tensor_scalar(away, tile_no[:, 0:n], float(P), -float(PAD_ROW), ALU.mult, ALU.add))
                chain.link(V.tensor_tensor(away, away, used, ALU.mult))
                chain.link(V.tensor_tensor(base, base, away, ALU.add))
                chain.link(V.tensor_scalar(base, base, float(PAD_ROW), None, ALU.add))
                chain.link(V.tensor_copy(row_tab[:, t0:t1], base))
                chain.link(V.tensor_tensor(s1, s0, by_tile(expert8[:, :]), ALU.mult))
                chain.link(V.tensor_reduce(number, s1, AX.X, ALU.add))
                chain.link(V.tensor_scalar(number, number, float(NE), float(NE - 1), ALU.add, ALU.min))
                V.tensor_copy(expert_tab[:, t0:t1], number).then_inc(tables_ready, 1)

            def run(b, order, const, per):
                for name, g, u, unit, units_ready in numbered(order, const):
                    G = b * NG + g
                    s = slot(unit or 0)
                    ready = units_ready + b * per
                    if name in ("Q", "K"):
                        i = int(name == "K")
                        two = projected(b, g) * 2 + i
                        dve.wait_ge(high_ready[u], two + 1)
                        wait(dve, low_ready[u], two)
                        V.tensor_tensor(rest[:, u, :], pa[:, s, :], parts[i][0][:, u, :], ALU.subtract)\
                            .then_inc(unit_read[s], 1)
                        wait_read(dve, unit, b, per)
                        V.tensor_copy(parts[i][1][:, u, :], rest[:, u, :]).then_inc(mid_ready[u], 1)
                    elif name == "W":
                        w = projections[u][0]
                        dve.wait_ge(raw_in[u], 16)
                        V.tensor_copy(w[:, 0].bitcast(F32R), raw[u]).then_inc(high_weights, 1)
                        dve.wait_ge(high_weights, u + 1)
                        V.tensor_tensor(w[:, 1].bitcast(F32R), raw[u], w[:, 0], ALU.subtract).then_inc(weights_split, 1)
                    elif name == "XS" and order is PROLOGUE:
                        dve.wait_ge(xT_high, 1)
                        V.tensor_tensor(xT[:, 1].bitcast(F32R), x_in[:], xT[:, 0], ALU.subtract).then_inc(xT_low, 1)
                    elif name in ("C", "YT"):
                        high_part, dst = (cT_high, cT) if name == "C" else (yT_high, yT)
                        dve.wait_ge(high_part, past(b, g) * 2 - 1 + u if name == "YT" else projected(b, g) + 1)
                        V.tensor_tensor(dst[:, 1, u].bitcast(F32R), pa[:, s, :], dst[:, 0, u], ALU.subtract)\
                            .then_inc(unit_read[s], 1)
                    elif name == "S":
                        dve.wait_ge(unit_ready, ready)
                        if u < 2:
                            V.tensor_reduce(row_max[:, 2 * u:2 * u + 2, 1], pa[:, s, :].rearrange("p (h t) -> p h t", h=2),
                                            AX.X, ALU.max).then_inc(unit_read[s], 1)
                        elif u < 6:
                            V.tensor_reduce(row_max[:, u - 2, 2:3], pa[:, s, 0:3 * P], AX.X, ALU.max)
                            V.tensor_reduce(row_max[:, u - 2, 0:1], pa[:, s, 3 * P:T], AX.X, ALU.max)\
                                .then_inc(unit_read[s], 1)
                        else:
                            V.tensor_reduce(row_max[:, u - 6, 3:4], pa[:, s, :], AX.X, ALU.max).then_inc(unit_read[s], 1)
                        if u == 9:
                            wait_read(dve, unit, b, per)
                            high, mid, low = (max_parts[:, i, :, :] for i in range(3))
                            chain.link(V.tensor_scalar(high, row_max[:], -1.0, None, ALU.mult))
                            chain.link(V.scalar_tensor_tensor(max_rest[:], row_max[:], -1.0, high, ALU.mult, ALU.subtract))
                            chain.link(V.tensor_copy(mid, max_rest[:]))
                            V.tensor_tensor(low, max_rest[:], mid, ALU.subtract).then_inc(max_parts_ready, 1)
                    elif name == "OT":
                        dve.wait_ge(unit_ready, ready)
                        o4 = pa[:, s, :].rearrange("p (t h d) -> p t h d", t=TT, h=GH)
                        chain.link(V.reciprocal(rsum[:, g % 2], o4[:, :, :, HS]))
                        ch = (g - 1) % NG * GH * HS
                        y4 = y[:, :, ch:ch + GH * HS].rearrange("p t (h d) -> p t h d", h=GH)
                        V.tensor_tensor(y4, o4[:, :, :, 0:HS],
                                        rsum[:, g % 2].rearrange("p t (h o) -> p t h o", o=1).to_broadcast([P, TT, GH, HS]),
                                        ALU.mult).then_inc(unit_read[s], 1)
                    elif name == "WO":
                        dve.wait_ge(unit_ready, ready)
                        dve.wait_ge(xr_biased, past(b, g))
                        half = xr[:, 2 * u:2 * u + 2, 0:C]
                        V.tensor_tensor(half, pa[:, s, :].rearrange("p (t c) -> p t c", t=2), half, ALU.add)\
                            .then_inc(unit_read[s], 1)
                        summed = unit
                    elif name == "ST":
                        wait_read(dve, summed, b, per)
                        for t in range(TT):
                            last = V.bn_stats(stats[:, t, :], xr[:, t, 0:C])
                        chain.link(last)
                        apart(dve)
                        for t in range(TT):
                            last = V.bn_aggr(mean_var[:, t, :], stats[:, t, :])
                        last.then_inc(var_ready, 1)
                    elif name == "LN":
                        dve.wait_ge(rstd_ready, past(b, g))
                        for t in range(TT):
                            last = V.tensor_scalar(xr[:, t, 0:C], xr[:, t, 0:C], mean_var[:, t, 0:1], rstd[:, t:t + 1],
                                                   ALU.subtract, ALU.mult)
                        last.then_inc(x1_ready, 1)
                    elif name == "R" and u == 0:
                        first_half = unit
                    elif name == "R":
                        wait_read(dve, first_half, b, per)
                        apart(dve)
                        wait_read(dve, unit, b, per)
                        chain.link(V.tensor_scalar(route[:], route[:], 1.0, None, ALU.add))
                        chain.link(V.reciprocal(route[:], route[:]))
                        chain.link(V.tensor_reduce(xr[:, :, C], route[:], AX.X, ALU.max))
                        chain.link(V.tensor_tensor(pick[:], route[:],
                                                   xr[:, :, C:C + 1].to_broadcast([P, TT, NE]), ALU.is_equal))
                        e8 = expert8[:, :].rearrange("p (o e) -> p o e", o=1).to_broadcast([P, TT, NE])
                        chain.link(V.tensor_tensor(pick[:], pick[:], e8, ALU.mult))
                        chain.link(V.tensor_reduce(pick_min[:], pick[:], AX.X, ALU.min))
                        V.tensor_tensor(onehot[:], e8, pick_min[:, :].rearrange("p (t o) -> p t o", o=1)
                                        .to_broadcast([P, TT, NE]), ALU.is_equal).then_inc(onehot_ready, 1)
                    elif name == "RK":
                        dve.wait_ge(unit_ready, ready)
                        ranks = pa[:, s, 0:(TT + 1) * NE].rearrange("p (t e) -> p t e", e=NE)
                        nr = next_row[:, :].rearrange("p (o e) -> p o e", o=1)
                        chain.link(V.tensor_tensor(place[:], ranks[:, 0:TT, :], nr.to_broadcast([P, TT, NE]), ALU.add))
                        chain.link(V.tensor_tensor(place[:], place[:], onehot[:], ALU.mult))
                        V.tensor_tensor(nr, ranks[:, TT:TT + 1, :], nr, ALU.add).then_inc(unit_read[s], 1)
                        chain.link(V.tensor_reduce(dest[:], place[:], AX.X, ALU.add))
                        chain.link(V.tensor_copy(xr[:, :, C + 1], token_no[:]))
                        chain.link(V.tensor_scalar(token_no[:], token_no[:], float(T), None, ALU.add))
                        V.tensor_copy(dest_i[:], dest[:]).then_inc(dest_ready, 1)
                        if order is EPILOGUE:
                            V.tensor_copy(pad_tab[:], next_row[:]).then_inc(ends_ready, 1)
                    elif name in ("TE", "TL"):
                        make_tables(early=name == "TE")
                    elif name == "F0":
                        first_step(*tile(0, 0, u), outer_too=u > 1)
                    elif name == "F1":
                        second_step(*tile(0, 0, u), norm_too=u > 1)
                    elif name == "FE":
                        for k in range(-2, 0):
                            outer(*tile(0, 0, EARLY + k))
                            norm(*tile(0, 0, EARLY + k))

            V.memset(vv[:], 1.0).then_inc(vv_ones, 1)
            V.memset(padding[:, 0:C + 1], 0.0)
            V.memset(padding[:, C + 1:ROW], NO_TOKEN)
            V.memset(minus_half[:], -0.5)
            V.memset(one8[:], 1.0).then_inc(ones_done, 1)
            dve.wait_ge(ones_done, 1)
            dve.wait_ge(const_done, 1)
            chain.link(V.tensor_scalar(region0[:], expert8[:], float(NE), float(REGION), ALU.add, ALU.mult))
            chain.link(V.tensor_copy(next_row[:], region0[:]))

            run(0, PROLOGUE, U0, 0)
            bodies(chain.counted(run), dve.Fori)
            run(NB - 1, EPILOGUE, U_END, 0)

            first_step(*tile(0, 0, EARLY), outer_too=False)
            second_step(*tile(0, 0, EARLY), norm_too=False)
            first_step(*tile(0, 0, EARLY + 1), outer_too=False)
            second_step(*tile(0, 0, EARLY + 1), norm_too=False)
            with dve.Fori(EARLY // 2 + 1, NT // 2) as p:
                for k in range(2):
                    first_step(*tile(p, 1, k))
                    second_step(*tile(p, 1, k))
            for k in range(-1, 1):
                outer(*tile(NT // 2, 0, k))
                norm(*tile(NT // 2, 0, k))

        @block.gpsimd
        def _(pool):
            g_ = nc.gpsimd
            chain = Chain(pool, pool_chain, POOL_LINKS)
            g_.memset(ident[:], 0.0)
            g_.memset(ident_b[:], 0.0)
            g_.memset(causal[:], 0.0)
            g_.memset(earlier[:], 1.0)
            g_.memset(ones_b[:], 1.0)
            g_.iota(expert8[:], [[1, NE]], base=-NE, channel_multiplier=0, allow_small_or_imprecise_dtypes=True)
            g_.iota(tile_no[:], [[1, NT]], base=0, channel_multiplier=0, allow_small_or_imprecise_dtypes=True)
            chain.link(g_.iota(token_no[:], [[P, TT]], base=0, channel_multiplier=1,
                               allow_small_or_imprecise_dtypes=True))
            for m in (ident, ident_b):
                g_.affine_select(out=m[:], in_=m[:], pattern=[[-1, P]], compare_op=ALU.not_equal, fill=1.0,
                                 base=0, channel_multiplier=1)
            g_.affine_select(out=causal[:], in_=causal[:], pattern=[[-1, P]], compare_op=ALU.is_ge, fill=MASKED,
                             base=0, channel_multiplier=1)
            g_.affine_select(out=earlier[:], in_=earlier[:], pattern=[[1, P]], compare_op=ALU.is_gt, fill=0.0,
                             base=0, channel_multiplier=-1).then_inc(const_done, 1)

            pool.wait_ge(const_done, 1)
            g_.memset(k_stack[KS:KM, :, :], 1.0).then_inc(stack_ones, 1)

            def clear_later(view, blocks):
                return g_.affine_select(out=view, in_=view, pattern=[[0, k] for k in blocks] + [[1, P]],
                                        compare_op=ALU.is_ge, fill=0.0, base=0, channel_multiplier=-1)

            def finish(pair, odd):
                i = 2 * pair + odd
                pool.wait_ge(zvar_ready, i + 1)
                apart(pool)
                g_.tensor_scalar(zrstd[:, odd:odd + 1], zmv[:, odd, 1:2], EPS, None, ALU.add).then_inc(zeps_ready, 1)
                pool.wait_ge(zeps_ready, i + 1)
                g_.tensor_tensor(zrstd[:, odd:odd + 1], zrstd[:, odd:odd + 1], minus_half[:, 0:1], ALU.pow)\
                    .then_inc(zrstd_ready, 1)
                pool.wait_ge(z_normed, i + 1)
                apart(pool)
                g_.indirect_dma_start(out=out_rows, out_offset=bass.IndirectOffsetOnAxis(zi[:, odd:odd + 1], 0),
                                      in_=z[:, odd, :], in_offset=None, bounds_check=NTOK - 1, oob_is_err=False)\
                    .then_inc(out_done[odd], 16)

            def run(b, order, const, per):
                for name, g, u in order:
                    G = b * NG + g
                    if name in ("QL", "KL"):
                        i = int(name == "KL")
                        pool.wait_ge(mid_ready[u], projected(b, g) * 2 + i + 1)
                        g_.tensor_tensor(parts[i][2][:, u, :], rest[:, u, :], parts[i][1][:, u, :], ALU.subtract)\
                            .then_inc(low_ready[u], 1)
                    elif name == "XS" and order is not PROLOGUE:
                        pool.wait_ge(xT_high, projected(b, g) + 1)
                        apart(pool)
                        g_.tensor_tensor(xT[:, 1].bitcast(F32R), x_in[:], xT[:, 0], ALU.subtract).then_inc(xT_low, 1)
                    elif name == "B" and u in (3, 7, 9):
                        pool.wait_ge(exp_done, G * BANKS + u + 1)
                        apart(pool)
                        if u == 3:
                            last = clear_later(probs[:, 0:4, 0:P], [GH])
                        elif u == 7:
                            view = probs[:, 4:8, :].rearrange("p h (k q) -> p h k q", q=P)
                            clear_later(view[:, :, 0, :], [GH])
                            last = clear_later(view[:, :, 3, :], [GH])
                        else:
                            view = probs[:, 8:10, :].rearrange("p h (k q) -> p (h k) q", q=2 * P)
                            last = clear_later(view[:, :, 0:P], [GH])
                        last.then_inc(masked, 1)
                    elif name == "XB":
                        pool.wait_ge(xr_in, (past(b, g)) * 16)
                        g_.tensor_tensor(xr[:, :, 0:C], xr[:, :, 0:C],
                                         bias[:, :].rearrange("p (o c) -> p o c", o=1).to_broadcast([P, TT, C]),
                                         ALU.add).then_inc(xr_biased, 1)
                    elif name == "RV":
                        pool.wait_ge(var_ready, past(b, g))
                        apart(pool)
                        chain.link(g_.tensor_scalar(rstd[:], mean_var[:, :, 1], EPS, None, ALU.add))
                        g_.tensor_tensor(rstd[:], rstd[:], minus_half[:], ALU.pow).then_inc(rstd_ready, 1)
                    elif name == "SC":
                        if u == 0:
                            pool.wait_ge(dest_ready, past(b, g))
                            apart(pool)
                        g_.indirect_dma_start(out=rows_dram, out_offset=bass.IndirectOffsetOnAxis(dest_i[:, u:u + 1], 0),
                                              in_=xr[:, u, :], in_offset=None).then_inc(scattered, 16)
                    elif name == "F1" and u > 1:
                        finish(*tile(0, 0, u - 2))
                    elif name == "FE":
                        for k in range(-2, 0):
                            finish(*tile(0, 0, EARLY + k))

            pool.wait_ge(stack_ones, 1)
            pool.wait_ge(weights_in, 2 * 16)
            run(0, PROLOGUE, U0, 0)
            bodies(chain.counted(run), pool.Fori)
            run(NB - 1, EPILOGUE, U_END, 0)

            with pool.Fori(EARLY // 2, NT // 2) as p:
                finish(p, 1)
                finish(p + 1, 0)


_INS = ["L0_attn_x", "x_turned", "L0_attn_Wq", "L0_attn_Wc", "L0_attn_Wk", "L0_attn_Wv", "L0_attn_Wo", "L0_attn_bo",
        "L0_ffn_router_w", "L0_ffn_gate_w", "L0_ffn_up_w", "L0_ffn_down_w"]


def kernel(**inputs):
    import numpy as np
    import concourse.bacc as bacc
    from concourse.bass_utils import run_bass_kernel_spmd

    nc = bacc.Bacc("TRN2", target_bir_lowering=False, num_devices=1)
    arrays, args = {}, []
    inputs["x_turned"] = np.asarray(inputs["L0_attn_x"]).transpose(0, 2, 1)
    for name in _INS:
        a = inputs[name]
        if name in ("L0_attn_Wq", "L0_attn_Wk"):
            a = np.asarray(a).reshape(-1, NG, GH, HS).transpose(0, 1, 3, 2).reshape(-1, C)
        a = np.ascontiguousarray(a)
        arrays[name + "_dram"] = a
        args.append(nc.dram_tensor(name + "_dram", a.shape, mybir.dt.from_np(a.dtype), kind="ExternalInput").ap())
    args.append(nc.dram_tensor("out_dram", (NB, T, C), F32, kind="ExternalOutput").ap())
    kernel_program(nc, *args)
    return run_bass_kernel_spmd(nc, [arrays], core_ids=[0]).results[0]["out_dram"]
```
